# Optimizing a Trainium2 kernel written in Bass

```python
import numpy as np
import jax
import jax.numpy as jnp

def _softmax(x, axis=-1):
    return jax.nn.softmax(x, axis=axis)

def _gelu(x):
    return jax.nn.gelu(x, approximate=True)

def _silu(x):
    return jax.nn.silu(x)

def _sigmoid(x):
    return jax.nn.sigmoid(x)

def _layernorm(x, axis=-1, eps=1e-05):
    m = jnp.mean(x, axis=axis, keepdims=True)
    v = jnp.var(x, axis=axis, keepdims=True)
    return (x - m) / jnp.sqrt(v + eps)

def _scatter_add(tgt, idx, src, axis=0):
    return tgt.at[idx].add(src)

def _segment_sum(src, seg, n):
    return jax.ops.segment_sum(src, seg, n)
kernel_name = 'mk_dlrm_tower_d1_rec_r8_758a94'

def setup_inputs(seed: int=0):
    np.random.seed(seed)
    _w = jnp.asarray

    def _rec_inputs():
        import jax
        import jax.numpy as jnp
        _tk = jax.random.key(seed)
        dense_ctx = jax.random.normal(jax.random.fold_in(_tk, 190), (2048, 16), jnp.float32)
        ids = jnp.stack([jax.random.randint(jax.random.fold_in(_tk, 200 + f), (2048,), 0, v, jnp.int32) for f, v in enumerate([1000, 1250, 1000, 12500, 12500, 1000, 1000, 1000, 12500, 12500, 1000, 125000, 1250, 125000, 1000, 1250, 1250, 1250, 125000, 12500, 1000, 12500, 1250, 1000, 1000, 12500, 1000, 1000, 1000, 12500, 1000, 1000, 1000, 1000, 1000, 1000, 1000, 1250, 1250, 1000])], axis=1)
        tbl_0 = 0.05 * jax.random.normal(jax.random.fold_in(_tk, 500 + 0), (1000, 64), jnp.float32)
        tbl_1 = 0.05 * jax.random.normal(jax.random.fold_in(_tk, 500 + 1), (1250, 64), jnp.float32)
        tbl_2 = 0.05 * jax.random.normal(jax.random.fold_in(_tk, 500 + 2), (1000, 64), jnp.float32)
        tbl_3 = 0.05 * jax.random.normal(jax.random.fold_in(_tk, 500 + 3), (12500, 64), jnp.float32)
        tbl_4 = 0.05 * jax.random.normal(jax.random.fold_in(_tk, 500 + 4), (12500, 64), jnp.float32)
        tbl_5 = 0.05 * jax.random.normal(jax.random.fold_in(_tk, 500 + 5), (1000, 64), jnp.float32)
        tbl_6 = 0.05 * jax.random.normal(jax.random.fold_in(_tk, 500 + 6), (1000, 64), jnp.float32)
        tbl_7 = 0.05 * jax.random.normal(jax.random.fold_in(_tk, 500 + 7), (1000, 64), jnp.float32)
        tbl_8 = 0.05 * jax.random.normal(jax.random.fold_in(_tk, 500 + 8), (12500, 64), jnp.float32)
        tbl_9 = 0.05 * jax.random.normal(jax.random.fold_in(_tk, 500 + 9), (12500, 64), jnp.float32)
        tbl_10 = 0.05 * jax.random.normal(jax.random.fold_in(_tk, 500 + 10), (1000, 64), jnp.float32)
        tbl_11 = 0.05 * jax.random.normal(jax.random.fold_in(_tk, 500 + 11), (125000, 64), jnp.float32)
        tbl_12 = 0.05 * jax.random.normal(jax.random.fold_in(_tk, 500 + 12), (1250, 64), jnp.float32)
        tbl_13 = 0.05 * jax.random.normal(jax.random.fold_in(_tk, 500 + 13), (125000, 64), jnp.float32)
        tbl_14 = 0.05 * jax.random.normal(jax.random.fold_in(_tk, 500 + 14), (1000, 64), jnp.float32)
        tbl_15 = 0.05 * jax.random.normal(jax.random.fold_in(_tk, 500 + 15), (1250, 64), jnp.float32)
        tbl_16 = 0.05 * jax.random.normal(jax.random.fold_in(_tk, 500 + 16), (1250, 64), jnp.float32)
        tbl_17 = 0.05 * jax.random.normal(jax.random.fold_in(_tk, 500 + 17), (1250, 64), jnp.float32)
        tbl_18 = 0.05 * jax.random.normal(jax.random.fold_in(_tk, 500 + 18), (125000, 64), jnp.float32)
        tbl_19 = 0.05 * jax.random.normal(jax.random.fold_in(_tk, 500 + 19), (12500, 64), jnp.float32)
        tbl_20 = 0.05 * jax.random.normal(jax.random.fold_in(_tk, 500 + 20), (1000, 64), jnp.float32)
        tbl_21 = 0.05 * jax.random.normal(jax.random.fold_in(_tk, 500 + 21), (12500, 64), jnp.float32)
        tbl_22 = 0.05 * jax.random.normal(jax.random.fold_in(_tk, 500 + 22), (1250, 64), jnp.float32)
        tbl_23 = 0.05 * jax.random.normal(jax.random.fold_in(_tk, 500 + 23), (1000, 64), jnp.float32)
        tbl_24 = 0.05 * jax.random.normal(jax.random.fold_in(_tk, 500 + 24), (1000, 64), jnp.float32)
        tbl_25 = 0.05 * jax.random.normal(jax.random.fold_in(_tk, 500 + 25), (12500, 64), jnp.float32)
        tbl_26 = 0.05 * jax.random.normal(jax.random.fold_in(_tk, 500 + 26), (1000, 64), jnp.float32)
        tbl_27 = 0.05 * jax.random.normal(jax.random.fold_in(_tk, 500 + 27), (1000, 64), jnp.float32)
        tbl_28 = 0.05 * jax.random.normal(jax.random.fold_in(_tk, 500 + 28), (1000, 64), jnp.float32)
        tbl_29 = 0.05 * jax.random.normal(jax.random.fold_in(_tk, 500 + 29), (12500, 64), jnp.float32)
        tbl_30 = 0.05 * jax.random.normal(jax.random.fold_in(_tk, 500 + 30), (1000, 64), jnp.float32)
        tbl_31 = 0.05 * jax.random.normal(jax.random.fold_in(_tk, 500 + 31), (1000, 64), jnp.float32)
        tbl_32 = 0.05 * jax.random.normal(jax.random.fold_in(_tk, 500 + 32), (1000, 64), jnp.float32)
        tbl_33 = 0.05 * jax.random.normal(jax.random.fold_in(_tk, 500 + 33), (1000, 64), jnp.float32)
        tbl_34 = 0.05 * jax.random.normal(jax.random.fold_in(_tk, 500 + 34), (1000, 64), jnp.float32)
        tbl_35 = 0.05 * jax.random.normal(jax.random.fold_in(_tk, 500 + 35), (1000, 64), jnp.float32)
        tbl_36 = 0.05 * jax.random.normal(jax.random.fold_in(_tk, 500 + 36), (1000, 64), jnp.float32)
        tbl_37 = 0.05 * jax.random.normal(jax.random.fold_in(_tk, 500 + 37), (1250, 64), jnp.float32)
        tbl_38 = 0.05 * jax.random.normal(jax.random.fold_in(_tk, 500 + 38), (1250, 64), jnp.float32)
        tbl_39 = 0.05 * jax.random.normal(jax.random.fold_in(_tk, 500 + 39), (1000, 64), jnp.float32)
        _rk = jax.random.fold_in(_tk, 7)
        W_top1 = 0.0354441 * jax.random.normal(jax.random.fold_in(_tk, 801), (796, 512), jnp.float32)
        W_top2 = 0.0441942 * jax.random.normal(jax.random.fold_in(_tk, 802), (512, 256), jnp.float32)
        W_top3 = 0.0625 * jax.random.normal(jax.random.fold_in(_tk, 803), (256, 1), jnp.float32)
        b_top1 = jnp.zeros((512,), jnp.float32)
        b_top2 = jnp.zeros((256,), jnp.float32)
        return (dense_ctx, ids, tbl_0, tbl_1, tbl_2, tbl_3, tbl_4, tbl_5, tbl_6, tbl_7, tbl_8, tbl_9, tbl_10, tbl_11, tbl_12, tbl_13, tbl_14, tbl_15, tbl_16, tbl_17, tbl_18, tbl_19, tbl_20, tbl_21, tbl_22, tbl_23, tbl_24, tbl_25, tbl_26, tbl_27, tbl_28, tbl_29, tbl_30, tbl_31, tbl_32, tbl_33, tbl_34, tbl_35, tbl_36, tbl_37, tbl_38, tbl_39, W_top1, b_top1, W_top2, b_top2, W_top3)
    dense_ctx, ids, tbl_0, tbl_1, tbl_2, tbl_3, tbl_4, tbl_5, tbl_6, tbl_7, tbl_8, tbl_9, tbl_10, tbl_11, tbl_12, tbl_13, tbl_14, tbl_15, tbl_16, tbl_17, tbl_18, tbl_19, tbl_20, tbl_21, tbl_22, tbl_23, tbl_24, tbl_25, tbl_26, tbl_27, tbl_28, tbl_29, tbl_30, tbl_31, tbl_32, tbl_33, tbl_34, tbl_35, tbl_36, tbl_37, tbl_38, tbl_39, W_top1, b_top1, W_top2, b_top2, W_top3 = _rec_inputs()

    def _L0_rec_setup():
        import jax, jax.numpy as jnp
        import numpy as np

        def _pair_indices(num_fields):
            i_idx, j_idx = np.triu_indices(num_fields, k=1)
            return (jnp.asarray(i_idx), jnp.asarray(j_idx))
        key = jax.random.key(seed)
        k1, k2 = jax.random.split(key)
        B, F, D = (256, 40, 64)
        P = F * (F - 1) // 2
        x = jax.random.normal(k1, (B, F, D), dtype=jnp.float32)
        W = jax.random.normal(k2, (P, D, D), dtype=jnp.float32) * (1.0 / np.sqrt(D))
        return {'x': x, 'W': W}
    _L0_rec_all = _L0_rec_setup()
    _L0_rec_in = {k: v for k, v in _L0_rec_all.items() if k in ('W',)}
    del _L0_rec_all
    return {'dense_ctx': dense_ctx, 'ids': ids, 'tbl_0': tbl_0, 'tbl_1': tbl_1, 'tbl_2': tbl_2, 'tbl_3': tbl_3, 'tbl_4': tbl_4, 'tbl_5': tbl_5, 'tbl_6': tbl_6, 'tbl_7': tbl_7, 'tbl_8': tbl_8, 'tbl_9': tbl_9, 'tbl_10': tbl_10, 'tbl_11': tbl_11, 'tbl_12': tbl_12, 'tbl_13': tbl_13, 'tbl_14': tbl_14, 'tbl_15': tbl_15, 'tbl_16': tbl_16, 'tbl_17': tbl_17, 'tbl_18': tbl_18, 'tbl_19': tbl_19, 'tbl_20': tbl_20, 'tbl_21': tbl_21, 'tbl_22': tbl_22, 'tbl_23': tbl_23, 'tbl_24': tbl_24, 'tbl_25': tbl_25, 'tbl_26': tbl_26, 'tbl_27': tbl_27, 'tbl_28': tbl_28, 'tbl_29': tbl_29, 'tbl_30': tbl_30, 'tbl_31': tbl_31, 'tbl_32': tbl_32, 'tbl_33': tbl_33, 'tbl_34': tbl_34, 'tbl_35': tbl_35, 'tbl_36': tbl_36, 'tbl_37': tbl_37, 'tbl_38': tbl_38, 'tbl_39': tbl_39, 'W_top1': W_top1, 'b_top1': b_top1, 'W_top2': W_top2, 'b_top2': b_top2, 'W_top3': W_top3, 'L0_rec_W': _L0_rec_in['W']}

def reference(dense_ctx, ids, tbl_0, tbl_1, tbl_2, tbl_3, tbl_4, tbl_5, tbl_6, tbl_7, tbl_8, tbl_9, tbl_10, tbl_11, tbl_12, tbl_13, tbl_14, tbl_15, tbl_16, tbl_17, tbl_18, tbl_19, tbl_20, tbl_21, tbl_22, tbl_23, tbl_24, tbl_25, tbl_26, tbl_27, tbl_28, tbl_29, tbl_30, tbl_31, tbl_32, tbl_33, tbl_34, tbl_35, tbl_36, tbl_37, tbl_38, tbl_39, W_top1, b_top1, W_top2, b_top2, W_top3, L0_rec_W):
    import jax
    import jax.numpy as jnp

    def _L0_rec_ref(x, W):
        import jax, jax.numpy as jnp
        import numpy as np

        def _pair_indices(num_fields):
            i_idx, j_idx = np.triu_indices(num_fields, k=1)
            return (jnp.asarray(i_idx), jnp.asarray(j_idx))
        B, F, D = x.shape
        i_idx, j_idx = _pair_indices(F)
        vi = x[:, i_idx, :]
        vj = x[:, j_idx, :]
        viW = jnp.einsum('bpd,pde->bpe', vi, W)
        out = jnp.einsum('bpe,bpe->bp', viW, vj)
        return out
    e = jnp.stack([tbl_0[ids[:, 0]], tbl_1[ids[:, 1]], tbl_2[ids[:, 2]], tbl_3[ids[:, 3]], tbl_4[ids[:, 4]], tbl_5[ids[:, 5]], tbl_6[ids[:, 6]], tbl_7[ids[:, 7]], tbl_8[ids[:, 8]], tbl_9[ids[:, 9]], tbl_10[ids[:, 10]], tbl_11[ids[:, 11]], tbl_12[ids[:, 12]], tbl_13[ids[:, 13]], tbl_14[ids[:, 14]], tbl_15[ids[:, 15]], tbl_16[ids[:, 16]], tbl_17[ids[:, 17]], tbl_18[ids[:, 18]], tbl_19[ids[:, 19]], tbl_20[ids[:, 20]], tbl_21[ids[:, 21]], tbl_22[ids[:, 22]], tbl_23[ids[:, 23]], tbl_24[ids[:, 24]], tbl_25[ids[:, 25]], tbl_26[ids[:, 26]], tbl_27[ids[:, 27]], tbl_28[ids[:, 28]], tbl_29[ids[:, 29]], tbl_30[ids[:, 30]], tbl_31[ids[:, 31]], tbl_32[ids[:, 32]], tbl_33[ids[:, 33]], tbl_34[ids[:, 34]], tbl_35[ids[:, 35]], tbl_36[ids[:, 36]], tbl_37[ids[:, 37]], tbl_38[ids[:, 38]], tbl_39[ids[:, 39]]], axis=1)
    z = _L0_rec_ref(e, L0_rec_W)
    z = z.reshape(z.shape[0], -1)
    h = jnp.concatenate([z, dense_ctx], axis=1)
    h = jnp.maximum(h @ W_top1 + b_top1, 0.0)
    h = jnp.maximum(h @ W_top2 + b_top2, 0.0)
    y = h @ W_top3
    return y

_drawn_inputs = setup_inputs


def setup_inputs(seed=0):
    import zlib

    import numpy as np

    out = dict(_drawn_inputs(seed))
    spreads = {'b_top1': (0.0, 0.1), 'b_top2': (0.0, 0.1)}
    factors = {}
    for name, (base, spread) in spreads.items():
        noise = np.random.default_rng([zlib.crc32(name.encode()), seed]).standard_normal(out[name].shape)
        drawn = base * np.exp(spread * noise) if base else spread * noise
        out[name] = jnp.asarray(drawn.astype(out[name].dtype))
    for name, factor in factors.items():
        out[name] = (out[name] * factor).astype(out[name].dtype)
    return out
```

```python
from contextlib import ExitStack

import concourse.bass as bass
import numpy as np
from concourse import mybir

ALU = mybir.AluOpType
ACT = mybir.ActivationFunctionType
F32 = mybir.dt.float32
F32R = mybir.dt.float32r
I32 = mybir.dt.int32

P = 128
FIELDS, DIM = 40, 64
DUOS = FIELDS // 2
BLOCK = 512
SUB = BLOCK // P
CHUNK = 8
W_SLOTS = 5
STACK_DUOS = 3
PROD_SLOTS = 4
LOOK = 3

TILES = [(i, m) for i in range(FIELDS - 2, -1, -1) for m in range(DUOS - 1, (i + 1) // 2 - 1, -1)]
NT = len(TILES)
GROUPS = NT // 4
PAIRS2 = NT // 2
CHUNKS = NT // CHUNK
ZK = -(-NT // 64)
Z_LAST = NT - 64 * (ZK - 1)
DENSE_ROW = 96
FIRST_TILE = {i: min(t for t, (f, _) in enumerate(TILES) if f == i) for i in range(FIELDS - 1)}
LAST_TILE = {i: max(t for t, (f, _) in enumerate(TILES) if f == i) for i in range(FIELDS - 1)}


def pair_index(i, j):
    return i * (2 * FIELDS - i - 1) // 2 + j - i - 1


def z_place(t):
    k, r = divmod(t, 64)
    strips = 4 if k < ZK - 1 else 3
    return k, r % strips, 2 * (r // strips)


def duo_tiles_before(n):
    return n * n


def w1_rows(n_dense):
    rows = np.zeros((P, ZK), np.int32)
    for t, (i, m) in enumerate(TILES):
        k, strip, r = z_place(t)
        for par in range(2):
            j = 2 * m + par
            if j > i:
                rows[32 * strip + r + par, k] = pair_index(i, j)
    n_pairs = FIELDS * (FIELDS - 1) // 2
    rows[DENSE_ROW:DENSE_ROW + n_dense, ZK - 1] = n_pairs + np.arange(n_dense)
    return rows


def chunk_segments(c):
    out, t = [], CHUNK * c
    while t < CHUNK * (c + 1):
        i = TILES[t][0]
        n = min(LAST_TILE[i] + 1, CHUNK * (c + 1)) - t
        m_low = TILES[t + n - 1][1]
        out.append((t - CHUNK * c, i, m_low, n))
        t += n
    return out


def weight_place(t):
    c = t // CHUNK
    for pos, i, m_low, n in chunk_segments(c):
        if TILES[t][0] == i:
            return c % W_SLOTS, pos + TILES[t][1] - m_low
    raise AssertionError


def order_of_block(with_mlp):
    duo_at = {}
    for n in range(DUOS):
        g = duo_tiles_before(n) // 4 - LOOK
        if n >= STACK_DUOS:
            g = max(g, (duo_tiles_before(n - STACK_DUOS + 1) - 1) // 4 + 1)
        duo_at.setdefault(max(g, 0), []).append(("duo", n))
    mlp_at = {0: [("l1", 0)], 1: [("l1", 1)], 2: [("l1", 2)], 3: [("l1", 3)],
              5: [("l2", 0)], 6: [("l2", 1)], 8: [("l3", 0)], 9: [("l3", 1)]}
    out = []
    for g in range(GROUPS):
        out += duo_at.get(g, [])
        out.append(("main", g))
        if g:
            out.append(("sum", g - 1))
        if with_mlp:
            out += mlp_at.get(g, [])
        if g == GROUPS - 8:
            out.append(("dense",))
    return out + [("sum", GROUPS - 1)]


def fields_of(n):
    m = DUOS - 1 - n
    return [f for f in (2 * m + 1, 2 * m) if f < FIELDS - 1]


def turn_uses(order):
    uses, u = {}, 0
    for ev in order:
        if ev[0] == "duo":
            uses[("T", ev[1])] = u
            u += 1
            for f in fields_of(ev[1]):
                uses[("E", f)] = u
                u += 1
        elif ev[0] in ("l1", "l2", "l3", "dense"):
            uses[ev] = u
            u += 1
    return uses, u


def dlrm_tower(nc, dense_ctx, ids, tables, W_top1, b_top1, W_top2, b_top2, W_top3, W_pair,
               w1_row_ids, out):
    BATCH, N_DENSE = dense_ctx.shape
    H1, H2 = W_top2.shape
    M1, M2 = H1 // P, H2 // P
    NB = BATCH // BLOCK
    NS = BATCH // P
    assert M1 == 4 and M2 == 2 and GROUPS * 4 == NT and CHUNKS * CHUNK == NT

    order_first = order_of_block(False)
    order_later = order_of_block(True)
    uses_first, n_first = turn_uses(order_first)
    uses_later, n_later = turn_uses(order_later)
    assert all(n_first - uses_first["E", f] == n_later - uses_later["E", f] for f in range(6))
    assert n_later % 2 == 0

    def turns_before(b):
        return 0 if isinstance(b, int) and b == 0 else b * n_later + (n_first - n_later)

    with ExitStack() as ctx:
        def sb(name, shape, dt=F32):
            return ctx.enter_context(nc.sbuf_tensor(name, shape, dt))

        def psum(name, shape):
            return ctx.enter_context(nc.psum_tensor(name, shape, F32))

        def sem(name):
            return ctx.enter_context(nc.semaphore(name))

        u_ps = psum("u_ps", [P, 4, BLOCK])
        z_ps = psum("z_ps", [P, 2, BLOCK])
        turn_ps = psum("turn_ps", [P, 2, BLOCK])

        rows = sb("rows", [P, DUOS, SUB, P])
        halves = sb("halves", [P, STACK_DUOS, SUB, 2, 2 * DIM])
        x_exact = sb("x_exact", [P, DUOS, BLOCK])
        x_stack = sb("x_stack", [P, 2 * STACK_DUOS, 2, BLOCK], F32R)
        w_ring = sb("w_ring", [P, W_SLOTS, CHUNK * P], F32R)
        raw_or_h1 = sb("raw_or_h1", [P, 4, BLOCK])
        prod = sb("prod", [P, PROD_SLOTS, 2, BLOCK])
        z_sb = sb("z_sb", [P, ZK, BLOCK])
        h2_sb = sb("h2_sb", [P, M2, BLOCK])
        y_row = sb("y_row", [P, BLOCK])
        w1_sb = sb("w1_sb", [P, ZK, H1])
        w2_sb = sb("w2_sb", [P, M1, H2])
        w3_sb = sb("w3_sb", [P, M2])
        b1_sb = sb("b1_sb", [P, M1])
        b2_sb = sb("b2_sb", [P, M2])
        ident = sb("ident", [P, P])
        ones_both = sb("ones_both", [P, 62])
        ones_odd = sb("ones_odd", [P, 62])
        dense_all = sb("dense_all", [P, NS, N_DENSE])
        dense_blk = sb("dense_blk", [P, SUB, N_DENSE])
        ids_all = sb("ids_all", [P, NS, FIELDS], I32)
        ids_blk = [sb(f"ids_blk{h}", [P, SUB, FIELDS // 2], I32) for h in range(2)]
        w1_ids = sb("w1_ids", [P, ZK], I32)
        raw = raw_or_h1[0:DIM].rearrange("p a b -> p (a b)").rearrange("p (s c) -> p s c", s=2)
        h1_sb = raw_or_h1

        w_split = nc.dram_tensor("w_split", (CHUNKS, P, CHUNK * P), F32, kind="Internal").ap()

        ids_in = sem("ids_in")
        w1_ids_in = sem("w1_ids_in")
        dense_in = sem("dense_in")
        mlp_in = sem("mlp_in")
        w1_in = sem("w1_in")
        rows_in = [sem(f"rows_in{m}") for m in range(DUOS)]
        raw_in = [sem(f"raw_in{s}") for s in range(2)]
        w_in = [sem(f"w_in{s}") for s in range(W_SLOTS)]
        w_out = [sem(f"w_out{s}") for s in range(W_SLOTS)]
        ids_copied = sem("ids_copied")
        rows_free = sem("rows_free")
        ident_zero = sem("ident_zero")
        ident_done = sem("ident_done")
        ones_zero = sem("ones_zero")
        ones_done = sem("ones_done")
        whi_done = sem("whi_done")
        wlo_done = sem("wlo_done")
        hi_done = sem("hi_done")
        lo_done = sem("lo_done")
        dense_copied = sem("dense_copied")
        turned = sem("turned")
        turn_read = sem("turn_read")
        mains_done = sem("mains_done")
        prods_done = sem("prods_done")
        sums_done = sem("sums_done")
        z_read = sem("z_read")
        y_done = sem("y_done")
        y_out = sem("y_out")

        block = ctx.enter_context(nc.Block())

        @block.sync
        def _(sp):
            sp.dma_start(ids_all[:], ids.rearrange("(s p) f -> p s f", p=P)).then_inc(ids_in, 16)

            def load_raw(c):
                for pos, i, m_low, n in chunk_segments(c):
                    dst = raw[:, c % 2, pos * P:(pos + n) * P].rearrange("d (q e) -> d q e", e=DIM)
                    first, skip = 2 * m_low, 0
                    if first == i == 0:
                        sp.dma_start(dst[:, 0], W_pair[0]).then_inc(raw_in[c % 2], 16)
                        first, skip = 1, 1
                    lo = pair_index(i, first)
                    sp.dma_start(dst[:, skip:], W_pair[lo:lo + 2 * n - skip].rearrange(
                        "q d e -> d q e")).then_inc(raw_in[c % 2], 16)

            for c in range(CHUNKS + 1):
                if c < CHUNKS:
                    if c >= 2:
                        sp.wait_ge(wlo_done, c - 1)
                    load_raw(c)
                if c == 1:
                    sp.dma_start(w2_sb[:], W_top2.rearrange("(k p) n -> p k n", p=P)).then_inc(mlp_in, 16)
                    sp.dma_start(w3_sb[:], W_top3.rearrange("(k p) o -> p (k o)", p=P), allow_slow_non_contiguous=True).then_inc(mlp_in, 16)
                    sp.dma_start(b1_sb[:], b_top1.rearrange("(m p) -> p m", p=P), allow_slow_non_contiguous=True).then_inc(mlp_in, 16)
                    sp.dma_start(b2_sb[:], b_top2.rearrange("(m p) -> p m", p=P), allow_slow_non_contiguous=True).then_inc(mlp_in, 16)
                    sp.dma_start(w1_ids[:], w1_row_ids).then_inc(w1_ids_in, 16)
                    sp.dma_start(dense_all[:], dense_ctx.rearrange("(s p) f -> p s f", p=P)).then_inc(dense_in, 16)
                if c >= 1:
                    sp.wait_ge(wlo_done, c)
                    sp.dma_start(w_split[c - 1], w_ring[:, (c - 1) % W_SLOTS, :].bitcast(F32)).then_inc(
                        w_out[(c - 1) % W_SLOTS], 16)
            for s in range(W_SLOTS):
                sp.wait_ge(w_out[s], 16 * (CHUNKS // W_SLOTS))
            with sp.Fori(1, NB) as b:
                for c in range(CHUNKS):
                    freed = NT * b + CHUNK * (c + 1 - W_SLOTS)
                    sp.wait_ge(mains_done, freed)
                    sp.dma_start(w_ring[:, c % W_SLOTS, :].bitcast(F32), w_split[c]).then_inc(
                        w_in[c % W_SLOTS], 16)

        @block.gpsimd
        def _(pool):
            nc.gpsimd.memset(ident[:], 0.0).then_inc(ident_zero, 1)
            pool.wait_ge(ident_zero, 1)
            nc.gpsimd.affine_select(out=ident[:], in_=ident[:], compare_op=ALU.not_equal, fill=1.0,
                                    base=0, pattern=[[-1, P]], channel_multiplier=1).then_inc(ident_done, 1)

            def copy_ids(b, half):
                nc.gpsimd.tensor_copy(
                    ids_blk[half][:],
                    ids_all[:, bass.ds(b * SUB, SUB), (1 - half) * FIELDS // 2:(2 - half) * FIELDS // 2],
                ).then_inc(ids_copied, 1)
                pool.wait_ge(ids_copied, 2 * b + half + 1)

            def gather(n):
                m = DUOS - 1 - n
                half = n // (DUOS // 2)
                for par in (1, 0):
                    f = 2 * m + par
                    for s in range(SUB):
                        at = f - (1 - half) * FIELDS // 2
                        nc.gpsimd.indirect_dma_start(
                            rows[:, m, s, par * DIM:(par + 1) * DIM], None, tables[f],
                            bass.IndirectOffsetOnAxis(ap=ids_blk[half][:, s, at:at + 1], axis=0),
                        ).then_inc(rows_in[m], 16)

            def low_half(b, n):
                m = DUOS - 1 - n
                slot = halves[:, n % STACK_DUOS]
                pool.wait_ge(hi_done, DUOS * b + n + 1)
                nc.gpsimd.tensor_tensor(
                    slot[:, :, :, DIM:2 * DIM], rows[:, m].rearrange("p s (h d) -> p s h d", h=2),
                    slot[:, :, :, 0:DIM], ALU.subtract).then_inc(lo_done, 1)

            pool.wait_ge(ids_in, 16)
            for n in range(DUOS):
                if n % (DUOS // 2) == 0:
                    copy_ids(0, n // (DUOS // 2))
                gather(n)
                if n == 4:
                    pool.wait_ge(w1_ids_in, 16)
                    for k in range(ZK):
                        nc.gpsimd.indirect_dma_start(
                            w1_sb[:, k, :], None, W_top1,
                            bass.IndirectOffsetOnAxis(ap=w1_ids[:, k:k + 1], axis=0)).then_inc(w1_in, 16)
                if n >= 1:
                    low_half(0, n - 1)
            low_half(0, DUOS - 1)

            def gather_next(b, n, uses):
                m = DUOS - 1 - n
                if n % (DUOS // 2) == 0:
                    half = n // (DUOS // 2)
                    for k in range(DUOS // 2):
                        pool.wait_ge(rows_in[DUOS - 1 - half * (DUOS // 2) - k], 2 * SUB * 16 * b)
                    copy_ids(b, half)
                pool.wait_ge(turned, turns_before(b - 1) + uses["E", fields_of(n)[-1]] + 1)
                pool.wait_ge(lo_done, DUOS * (b - 1) + n + 1)
                pool.sem_inc(rows_free, 1)
                gather(n)

            for n in range(DUOS):
                gather_next(1, n, uses_first)
            with pool.Fori(1, NB - 1) as b:
                nxt = 0
                for n in range(DUOS):
                    low_half(b, n)
                    for _ in range(0 if n < 7 else 1 if n < 13 else 2):
                        gather_next(b + 1, nxt, uses_later)
                        nxt += 1
            for n in range(DUOS):
                low_half(NB - 1, n)

        @block.tensor
        def _(pe):
            def turn_bank(b, use):
                if not (isinstance(b, int) and b == 0 and use < 2):
                    pe.wait_ge(turn_read, turns_before(b) + use - 1)
                return turn_ps[:, (use + (n_first if not isinstance(b, int) or b else 0)) % 2, :]

            def duo(b, n, uses):
                m = DUOS - 1 - n
                bank = turn_bank(b, uses["T", n])
                pe.wait_ge(rows_in[m], 2 * SUB * 16 * (b + 1))
                for s in range(SUB):
                    op = pe.transpose(bank[:, s * P:(s + 1) * P], rows[:, m, s, :], ident[:])
                op.then_inc(turned, 1)
                for f in fields_of(n):
                    bank = turn_bank(b, uses["E", f])
                    if f == fields_of(n)[0]:
                        pe.wait_ge(lo_done, DUOS * b + n + 1)
                    for s in range(SUB):
                        op = pe.transpose(bank[:, s * P:(s + 1) * P],
                                          halves[:, n % STACK_DUOS, s, f % 2, :], ident[:])
                    op.then_inc(turned, 1)

            def main(b, g, uses):
                first = isinstance(b, int)
                for t in range(4 * g, 4 * g + 4):
                    i, m = TILES[t]
                    c = t // CHUNK
                    if t % CHUNK == 0:
                        if first:
                            pe.wait_ge(whi_done, c + 1)
                            pe.wait_ge(wlo_done, c + 1)
                        else:
                            pe.wait_ge(w_in[c % W_SLOTS],
                                       b * (16 * CHUNKS // W_SLOTS) + 16 * (c // W_SLOTS + 1 - CHUNKS // W_SLOTS))
                    if t == FIRST_TILE[i]:
                        pe.wait_ge(turn_read, turns_before(b) + uses["E", i] + 1)
                    if t % 2 == 0 and not (first and t < 4):
                        pe.wait_ge(prods_done, PAIRS2 * b + t // 2 - 1)
                    slot, pos = weight_place(t)
                    w = w_ring[:, slot, pos * P:(pos + 1) * P]
                    n = DUOS - 1 - i // 2
                    x = x_stack[:, 2 * (n % STACK_DUOS) + i % 2]
                    pe.matmul(u_ps[:, t % 4, :], w, x[:, 0, :], start=True, stop=False)
                    pe.matmul(u_ps[:, t % 4, :], w, x[:, 1, :], start=False, stop=True).then_inc(mains_done, 1)

            def sums(b, g):
                first = isinstance(b, int)
                for t in range(4 * g, 4 * g + 4):
                    i, m = TILES[t]
                    k, strip, row = z_place(t)
                    if t % 2 == 0:
                        pe.wait_ge(prods_done, PAIRS2 * b + t // 2 + 1)
                    if t == 64 * k and not (first and k < 2):
                        pe.wait_ge(z_read, ZK * b + (k - 1 if k else 0))
                    ones = ones_odd if i == 2 * m else ones_both
                    strips = 4 if k < ZK - 1 else 3
                    r = t - 64 * k
                    tiles = 64 if k < ZK - 1 else Z_LAST
                    op = pe.matmul(z_ps[32 * strip:32 * strip + 32, k % 2, :], ones[:, 30 - row:62 - row],
                                   prod[:, t // 2 % PROD_SLOTS, t % 2, :],
                                   start=(r < strips), stop=(r >= tiles - strips))
                op.then_inc(sums_done, 1)

            def mlp(b, ev, use):
                bank = turn_bank(b, use)
                if ev[0] == "l1":
                    if ev[1] == 0:
                        pe.wait_ge(z_read, ZK * b)
                        pe.wait_ge(turn_read, turns_before(b))
                        if isinstance(b, int) or True:
                            pe.wait_ge(w1_in, 16 * ZK)
                            pe.wait_ge(mlp_in, 64)
                    cols = slice(ev[1] * P, (ev[1] + 1) * P)
                    for k in range(ZK):
                        op = pe.matmul(bank, w1_sb[:, k, cols], z_sb[:, k, :], start=(k == 0), stop=(k == ZK - 1))
                elif ev[0] == "l2":
                    pe.wait_ge(turn_read, turns_before(b) + MLP_USE["l1", M1 - 1](b) + 1)
                    cols = slice(ev[1] * P, (ev[1] + 1) * P)
                    for k in range(M1):
                        op = pe.matmul(bank, w2_sb[:, k, cols], h1_sb[:, k, :], start=(k == 0), stop=(k == M1 - 1))
                else:
                    pe.wait_ge(turn_read, turns_before(b) + MLP_USE["l2", M2 - 1](b) + 1)
                    half = slice(ev[1] * BLOCK // 2, (ev[1] + 1) * BLOCK // 2)
                    for k in range(M2):
                        op = pe.matmul(bank[0:1, 0:BLOCK // 2], w3_sb[:, k:k + 1], h2_sb[:, k, half],
                                       start=(k == 0), stop=(k == M2 - 1))
                op.then_inc(turned, 1)

            def dense(b, use):
                bank = turn_bank(b, use)
                pe.wait_ge(dense_copied, b + 1)
                for s in range(SUB):
                    op = pe.transpose(bank[0:N_DENSE, s * P:(s + 1) * P], dense_blk[:, s, :], ident[:])
                op.then_inc(turned, 1)

            def run_block(b, order, uses):
                for ev in order:
                    if ev[0] == "duo":
                        duo(b, ev[1], uses)
                    elif ev[0] == "main":
                        main(b, ev[1], uses)
                    elif ev[0] == "sum":
                        sums(b, ev[1])
                    elif ev[0] == "dense":
                        dense(b, uses[ev])
                    else:
                        mlp(b, ev, uses[ev])

            MLP_USE = {ev: (lambda b, ev=ev: last_uses[ev] if isinstance(b, int) else uses_later[ev])
                       for ev in uses_later if ev[0] in ("l1", "l2")}
            pe.wait_ge(ident_done, 1)
            pe.wait_ge(ones_done, 1)
            run_block(0, order_first, uses_first)
            with pe.Fori(1, NB) as b:
                run_block(b, order_later, uses_later)
            for ev in LAST_MLP:
                mlp(NB, ev, last_uses[ev])

        @block.vector
        def _(dve):
            nc.vector.memset(ones_both[:], 0.0)
            nc.vector.memset(z_sb[DENSE_ROW:P, ZK - 1, :], 0.0).then_inc(ones_zero, 1)
            nc.vector.memset(ones_odd[:], 0.0).then_inc(ones_zero, 1)
            dve.wait_ge(ones_zero, 2)
            nc.vector.memset(ones_both[0:DIM, 30:31], 1.0)
            nc.vector.memset(ones_both[DIM:P, 31:32], 1.0)
            nc.vector.memset(ones_odd[DIM:P, 31:32], 1.0).then_inc(ones_done, 1)

            def weight_low(c):
                dve.wait_ge(whi_done, c + 1)
                slot = w_ring[:, c % W_SLOTS, :]
                nc.vector.tensor_tensor(slot[DIM:P], raw[:, c % 2, :], slot[0:DIM].bitcast(F32),
                                        ALU.subtract).then_inc(wlo_done, 1)

            def products(b, q, uses):
                first = isinstance(b, int)
                t = 2 * q
                if first and t % 4 == 0:
                    for c in WEIGHTS_AT.get(t // 4, []):
                        weight_low(c)
                for tt in (t, t + 1):
                    n = DUOS - 1 - TILES[tt][1]
                    if TILES[tt][0] == 2 * TILES[tt][1]:
                        dve.wait_ge(turn_read, turns_before(b) + uses["T", n] + 1)
                dve.wait_ge(mains_done, NT * b + t + 2)
                if not (first and q < PROD_SLOTS):
                    dve.wait_ge(sums_done, GROUPS * b + (q - PROD_SLOTS) // 2 + 1)
                n0, n1 = (DUOS - 1 - TILES[tt][1] for tt in (t, t + 1))
                bank = t % 4
                if n1 == n0 + 1:
                    op = nc.vector.tensor_tensor(prod[:, q % PROD_SLOTS], u_ps[:, bank:bank + 2, :],
                                                 x_exact[:, n0:n0 + 2, :], ALU.mult)
                else:
                    nc.vector.tensor_tensor(prod[:, q % PROD_SLOTS, 0], u_ps[:, bank, :], x_exact[:, n0, :], ALU.mult)
                    op = nc.vector.tensor_tensor(prod[:, q % PROD_SLOTS, 1], u_ps[:, bank + 1, :],
                                                 x_exact[:, n1, :], ALU.mult)
                op.then_inc(prods_done, 1)

            for q in range(PAIRS2):
                products(0, q, uses_first)
            with dve.Fori(1, NB) as b:
                for q in range(PAIRS2):
                    products(b, q, uses_later)

        @block.scalar
        def _(act):
            def weight_high(c):
                act.wait_ge(raw_in[c % 2], 16 * RAW_DMAS[c])
                if c >= W_SLOTS:
                    act.wait_ge(mains_done, CHUNK * (c - W_SLOTS + 1))
                    act.wait_ge(w_out[c % W_SLOTS], 16 * (c // W_SLOTS))
                nc.scalar.copy(w_ring[0:DIM, c % W_SLOTS, :], raw[:, c % 2, :]).then_inc(whi_done, 1)

            def high_half(b, n):
                m = DUOS - 1 - n
                act.wait_ge(rows_in[m], 2 * SUB * 16 * (b + 1))
                if n >= STACK_DUOS:
                    uses = uses_first if isinstance(b, int) else uses_later
                    act.wait_ge(turned, turns_before(b) + uses["E", fields_of(n - STACK_DUOS)[-1]] + 1)
                elif not isinstance(b, int):
                    held = max(h for h in range(DUOS) if h % STACK_DUOS == n)
                    act.wait_ge(turned, turns_before(b) - n_later + uses_later["E", fields_of(held)[-1]] + 1)
                nc.scalar.copy(halves[:, n % STACK_DUOS, :, :, 0:DIM].bitcast(F32R),
                               rows[:, m].rearrange("p s (h d) -> p s h d", h=2)).then_inc(hi_done, 1)

            def turn_bank(b, use):
                act.wait_ge(turned, turns_before(b) + use + 1)
                return turn_ps[:, (use + (n_first if not isinstance(b, int) or b else 0)) % 2, :]

            def duo(b, n, uses):
                first = isinstance(b, int)
                if not first and n + 2 < DUOS:
                    high_half(b, n + 2)
                bank = turn_bank(b, uses["T", n])
                if not first:
                    t = FIRST_TILE[0] + n
                    act.wait_ge(prods_done, PAIRS2 * (b - 1) + t // 2 + 1)
                nc.scalar.copy(x_exact[:, n, :], bank).then_inc(turn_read, 1)
                for f in fields_of(n):
                    bank = turn_bank(b, uses["E", f])
                    x = x_stack[:, 2 * (n % STACK_DUOS) + f % 2]
                    if n >= STACK_DUOS:
                        act.wait_ge(mains_done, NT * b + duo_tiles_before(n - STACK_DUOS + 1))
                    elif not first:
                        held = max(h for h in range(DUOS) if h % STACK_DUOS == n)
                        act.wait_ge(mains_done, NT * (b - 1) + duo_tiles_before(held + 1))
                    nc.scalar.copy(x[:, 0, :], bank)
                    nc.scalar.copy(x[0:DIM, 1, :], bank[DIM:P])
                    nc.scalar.copy(x[DIM:P, 1, :], bank[0:DIM]).then_inc(turn_read, 1)
                if first and n + 1 < DUOS:
                    high_half(b, n + 1)

            def move_z(b, k):
                act.wait_ge(sums_done, GROUPS * b + min(16 * (k + 1), GROUPS))
                if k < ZK - 1:
                    nc.scalar.copy(z_sb[:, k, :], z_ps[:, k % 2, :]).then_inc(z_read, 1)
                else:
                    nc.scalar.copy(z_sb[0:DENSE_ROW, k, :], z_ps[0:DENSE_ROW, k % 2, :]).then_inc(z_read, 1)

            def mlp(b, ev, use):
                bank = turn_bank(b, use)
                if ev[0] == "l1":
                    if ev[1] == 0:
                        act.wait_ge(wlo_done, CHUNKS)
                    nc.scalar.activation(h1_sb[:, ev[1], :], bank, ACT.Relu,
                                         bias=b1_sb[:, ev[1]:ev[1] + 1]).then_inc(turn_read, 1)
                elif ev[0] == "l2":
                    nc.scalar.activation(h2_sb[:, ev[1], :], bank, ACT.Relu,
                                         bias=b2_sb[:, ev[1]:ev[1] + 1]).then_inc(turn_read, 1)
                else:
                    half = slice(ev[1] * BLOCK // 2, (ev[1] + 1) * BLOCK // 2)
                    nc.scalar.copy(y_row[0:1, half], bank[0:1, 0:BLOCK // 2]).then_inc(turn_read, 1)
                    if ev[1] == 1:
                        act.wait_ge(turn_read, turns_before(b) + use + 1)
                        act.dma_start(out.rearrange("n o -> o n")[:, bass.ds((b - 1) * BLOCK, BLOCK)],
                                      y_row[0:1, :]).then_inc(y_out, 16)

            def dense(b, use):
                bank = turn_bank(b, use)
                if not isinstance(b, int):
                    act.wait_ge(y_out, 16 * b)
                nc.scalar.copy(z_sb[DENSE_ROW:DENSE_ROW + N_DENSE, ZK - 1, :], bank[0:N_DENSE]).then_inc(turn_read, 1)

            def copy_dense(b):
                if not isinstance(b, int):
                    act.wait_ge(turned, turns_before(b))
                nc.scalar.copy(dense_blk[:], dense_all[:, bass.ds(b * SUB, SUB), :]).then_inc(dense_copied, 1)

            def run_block(b, order, uses):
                high_half(b, 0)
                if not isinstance(b, int):
                    high_half(b, 1)
                for ev in order:
                    if ev[0] == "duo":
                        duo(b, ev[1], uses)
                    elif ev[0] == "main":
                        if isinstance(b, int):
                            for c in WEIGHTS_AT.get(ev[1] + 1, []):
                                weight_high(c)
                        if ev[1] == 12:
                            copy_dense(b)
                    elif ev[0] == "sum":
                        g = ev[1]
                        if g % 16 == 15 or g == GROUPS - 1:
                            move_z(b, g // 16)
                    elif ev[0] == "dense":
                        dense(b, uses[ev])
                    else:
                        mlp(b, ev, uses[ev])

            for c in WEIGHTS_AT[0]:
                weight_high(c)
            act.wait_ge(dense_in, 16)
            act.wait_ge(mlp_in, 64)
            act.wait_ge(ones_zero, 2)
            run_block(0, order_first, uses_first)
            with act.Fori(1, NB) as b:
                run_block(b, order_later, uses_later)
            for ev in LAST_MLP:
                mlp(NB, ev, last_uses[ev])
            act.wait_ge(y_out, 16 * NB)


WEIGHTS_AT = {}
for _c in range(CHUNKS):
    WEIGHTS_AT.setdefault(max(0, 2 * _c - 6), []).append(_c)
_dmas = [len(chunk_segments(c)) + (c == CHUNKS - 1 and False) for c in range(CHUNKS)]
for _c in range(CHUNKS):
    for _pos, _i, _m, _n in chunk_segments(_c):
        if _i == 0 and _m == 0:
            _dmas[_c] += 1
RAW_DMAS = [sum(_dmas[c % 2:c + 1:2]) for c in range(CHUNKS)]
LAST_MLP = [("l1", 0), ("l1", 1), ("l1", 2), ("l1", 3), ("l2", 0), ("l2", 1), ("l3", 0), ("l3", 1)]
last_uses = {ev: u for u, ev in enumerate(LAST_MLP)}


def kernel(**inputs):
    import concourse.bacc as bacc
    from concourse.bass_utils import run_bass_kernel_spmd

    nc = bacc.Bacc("TRN2", target_bir_lowering=False, num_devices=1)
    arrays = {}

    def dram(name, a):
        arrays[name] = np.ascontiguousarray(a)
        return nc.dram_tensor(name, a.shape, mybir.dt.from_np(arrays[name].dtype), kind="ExternalInput").ap()

    args = {k: dram("in_" + k, np.asarray(v)) for k, v in inputs.items()}
    tables = [args[f"tbl_{f}"] for f in range(FIELDS)]
    rows = dram("w1_row_ids", w1_rows(args["dense_ctx"].shape[1]))
    out = nc.dram_tensor("out_y", (args["dense_ctx"].shape[0], 1), F32, kind="ExternalOutput").ap()
    dlrm_tower(nc, args["dense_ctx"], args["ids"], tables, args["W_top1"], args["b_top1"], args["W_top2"],
               args["b_top2"], args["W_top3"], args["L0_rec_W"], rows, out)
    r = run_bass_kernel_spmd(nc, [arrays], core_ids=[0])
    return r.results[0]["out_y"]
```

```python
from contextlib import ExitStack

import concourse.bass as bass
import numpy as np
from concourse import mybir

ALU = mybir.AluOpType
ACT = mybir.ActivationFunctionType
F32 = mybir.dt.float32
F32R = mybir.dt.float32r
I32 = mybir.dt.int32

P = 128
FIELDS, DIM = 40, 64
DUOS = FIELDS // 2
BLOCK = 512
SUB = BLOCK // P
CHUNK = 8
W_SLOTS = 5
STACK_DUOS = 3
U_SLOTS = 3
PROD_SLOTS = 8
AHEAD = 13
LOOK = 2

TILES = [(i, m) for i in range(FIELDS - 2, -1, -1) for m in range(DUOS - 1, (i + 1) // 2 - 1, -1)]
NT = len(TILES)
GROUP = 8
GROUPS = NT // GROUP
PAIRS2 = NT // 2
CHUNKS = NT // CHUNK
K_GROUPS = 64 // GROUP
ZK = -(-NT // 64)
Z_LAST = NT - 64 * (ZK - 1)
DENSE_ROW = 96
FIRST_TILE = {i: min(t for t, (f, _) in enumerate(TILES) if f == i) for i in range(FIELDS - 1)}
LAST_TILE = {i: max(t for t, (f, _) in enumerate(TILES) if f == i) for i in range(FIELDS - 1)}


def pair_index(i, j):
    return i * (2 * FIELDS - i - 1) // 2 + j - i - 1


def z_place(t):
    k, r = divmod(t, 64)
    strips = 4 if k < ZK - 1 else 3
    return k, r % strips, 2 * (r // strips)


def duo_tiles_before(n):
    return n * n


def w1_rows(n_dense):
    rows = np.zeros((P, ZK), np.int32)
    for t, (i, m) in enumerate(TILES):
        k, strip, r = z_place(t)
        for par in range(2):
            j = 2 * m + par
            if j > i:
                rows[32 * strip + r + par, k] = pair_index(i, j)
    n_pairs = FIELDS * (FIELDS - 1) // 2
    rows[DENSE_ROW:DENSE_ROW + n_dense, ZK - 1] = n_pairs + np.arange(n_dense)
    return rows


def chunk_segments(c):
    out, t = [], CHUNK * c
    while t < CHUNK * (c + 1):
        i = TILES[t][0]
        n = min(LAST_TILE[i] + 1, CHUNK * (c + 1)) - t
        m_low = TILES[t + n - 1][1]
        out.append((t - CHUNK * c, i, m_low, n))
        t += n
    return out


def weight_place(t):
    c = t // CHUNK
    for pos, i, m_low, n in chunk_segments(c):
        if TILES[t][0] == i:
            return c % W_SLOTS, pos + TILES[t][1] - m_low
    raise AssertionError


DUO_AT = {}
for _n in range(DUOS):
    _g = duo_tiles_before(_n) // GROUP - LOOK
    if _n >= STACK_DUOS:
        _g = max(_g, (duo_tiles_before(_n - STACK_DUOS + 1) - 1) // GROUP + 1)
    assert _g <= duo_tiles_before(_n) // GROUP
    DUO_AT.setdefault(max(_g, 0), []).append(_n)


LOW_AT = {}
for _n in range(DUOS):
    _k = min(max(_n + 1, 4 + duo_tiles_before(_n) // 12), DUOS + AHEAD)
    LOW_AT.setdefault(_k, []).append(_n)


def order_of_block(with_mlp):
    mlp_at = {0: ("l1", 0), 1: ("l1", 1), 2: ("l1", 2), 3: ("l1", 3), 4: ("l2", 0), 5: ("l2", 1), 7: ("l3", 0)}
    out = []
    for g in range(GROUPS):
        duos = DUO_AT.get(g, [])
        for k, n in enumerate(duos):
            out.append(("duo", n))
            if k:
                out.append(("stack", n - 1))
        if duos:
            out.append(("stack", duos[-1]))
        out.append(("main", g))
        if g:
            out.append(("sum", g - 1))
        if with_mlp and g in mlp_at:
            out.append(mlp_at[g])
        if g == GROUPS - 4:
            out.append(("dense", 0))
    return out + [("sum", GROUPS - 1)]


def fields_of(n):
    m = DUOS - 1 - n
    return [f for f in (2 * m + 1, 2 * m) if f < FIELDS - 1]


def turn_uses(order):
    events = [ev for ev in order if ev[0] in ("duo", "l1", "l2", "l3", "dense")]
    return {ev: u for u, ev in enumerate(events)}


def dlrm_tower(nc, dense_ctx, ids, tables, W_top1, b_top1, W_top2, b_top2, W_top3, W_pair,
               w1_row_ids, out):
    BATCH, N_DENSE = dense_ctx.shape
    H1, H2 = W_top2.shape
    M1, M2 = H1 // P, H2 // P
    NB = BATCH // BLOCK
    NS = BATCH // P
    assert M1 == 4 and M2 == 2 and GROUPS * GROUP == NT and CHUNKS * CHUNK == NT

    order_first = order_of_block(False)
    order_later = order_of_block(True)
    uses_first, uses_later = turn_uses(order_first), turn_uses(order_later)
    uses_last = {ev: u for u, ev in enumerate(LAST_MLP)}
    n_first, n_later = len(uses_first), len(uses_later)

    def turns_before(b):
        return 0 if isinstance(b, int) and b == 0 else b * n_later + (n_first - n_later)

    with ExitStack() as ctx:
        def sb(name, shape, dt=F32):
            return ctx.enter_context(nc.sbuf_tensor(name, shape, dt))

        def psum(name, shape):
            return ctx.enter_context(nc.psum_tensor(name, shape, F32))

        def sem(name):
            return ctx.enter_context(nc.semaphore(name))

        u_ps = psum("u_ps", [P, 2 * U_SLOTS, BLOCK])
        z_ps = psum("z_ps", [P, BLOCK])
        turn_ps = psum("turn_ps", [P, BLOCK])

        rows = sb("rows", [P, DUOS, SUB, P])
        x_exact = sb("x_exact", [P, DUOS, BLOCK])
        x_stack = sb("x_stack", [P, 2 * STACK_DUOS, 2, BLOCK], F32R)
        w_ring = sb("w_ring", [P, W_SLOTS, CHUNK * P], F32R)
        raw_or_h1 = sb("raw_or_h1", [P, 4, BLOCK])
        prod = sb("prod", [P, PROD_SLOTS, 2, BLOCK])
        z_sb = sb("z_sb", [P, ZK, BLOCK])
        h2_sb = sb("h2_sb", [P, M2, BLOCK])
        y_row = sb("y_row", [P, BLOCK])
        w1_sb = sb("w1_sb", [P, ZK, H1])
        w2_sb = sb("w2_sb", [P, M1, H2])
        w3_sb = sb("w3_sb", [P, M2])
        b1_sb = sb("b1_sb", [P, M1])
        b2_sb = sb("b2_sb", [P, M2])
        ident = sb("ident", [P, P])
        ones_both = sb("ones_both", [P, 62])
        ones_odd = sb("ones_odd", [P, 62])
        dense_all = sb("dense_all", [P, NS, N_DENSE])
        dense_blk = sb("dense_blk", [P, SUB, N_DENSE])
        ids_all = sb("ids_all", [P, NS, FIELDS], I32)
        ids_blk = [sb(f"ids_blk{h}", [P, SUB, FIELDS // 2], I32) for h in range(2)]
        w1_ids = sb("w1_ids", [P, ZK], I32)
        raw = raw_or_h1[0:DIM].rearrange("p a b -> p (a b)").rearrange("p (s c) -> p s c", s=2)
        h1_sb = raw_or_h1

        w_split = nc.dram_tensor("w_split", (CHUNKS, P, CHUNK * P), F32, kind="Internal").ap()

        ids_in = sem("ids_in")
        w1_ids_in = sem("w1_ids_in")
        dense_in = sem("dense_in")
        mlp_in = sem("mlp_in")
        w1_in = sem("w1_in")
        rows_in = [sem(f"rows_in{m}") for m in range(DUOS)]
        raw_in = [sem(f"raw_in{s}") for s in range(2)]
        w_in = [sem(f"w_in{s}") for s in range(W_SLOTS)]
        w_out = [sem(f"w_out{s}") for s in range(W_SLOTS)]
        ids_copied = sem("ids_copied")
        rows_free = sem("rows_free")
        ident_zero = sem("ident_zero")
        ident_done = sem("ident_done")
        ones_zero = sem("ones_zero")
        ones_done = sem("ones_done")
        whi_done = sem("whi_done")
        wlo_done = sem("wlo_done")
        hi_done = sem("hi_done")
        lo_done = sem("lo_done")
        lo_odd_done = sem("lo_odd_done")
        dense_copied = sem("dense_copied")
        stack_done = sem("stack_done")
        turned = sem("turned")
        turn_read = sem("turn_read")
        mains_done = sem("mains_done")
        prods_done = sem("prods_done")
        sums_done = sem("sums_done")
        z_read = sem("z_read")
        y_done = sem("y_done")
        y_out = sem("y_out")

        block = ctx.enter_context(nc.Block())

        @block.sync
        def _(sp):
            sp.dma_start(ids_all[:], ids.rearrange("(s p) f -> p s f", p=P)).then_inc(ids_in, 16)

            def load_raw(c):
                for pos, i, m_low, n in chunk_segments(c):
                    dst = raw[:, c % 2, pos * P:(pos + n) * P].rearrange("d (q e) -> d q e", e=DIM)
                    first, skip = 2 * m_low, 0
                    if first == i == 0:
                        sp.dma_start(dst[:, 0], W_pair[0]).then_inc(raw_in[c % 2], 16)
                        first, skip = 1, 1
                    lo = pair_index(i, first)
                    sp.dma_start(dst[:, skip:], W_pair[lo:lo + 2 * n - skip].rearrange(
                        "q d e -> d q e")).then_inc(raw_in[c % 2], 16)

            for c in range(CHUNKS + 1):
                if c < CHUNKS:
                    if c >= 2:
                        sp.wait_ge(wlo_done, c - 1)
                    load_raw(c)
                if c == 1:
                    sp.dma_start(w2_sb[:], W_top2.rearrange("(k p) n -> p k n", p=P)).then_inc(mlp_in, 16)
                    sp.dma_start(w3_sb[:], W_top3.rearrange("(k p) o -> p (k o)", p=P), allow_slow_non_contiguous=True).then_inc(mlp_in, 16)
                    sp.dma_start(b1_sb[:], b_top1.rearrange("(m p) -> p m", p=P), allow_slow_non_contiguous=True).then_inc(mlp_in, 16)
                    sp.dma_start(b2_sb[:], b_top2.rearrange("(m p) -> p m", p=P), allow_slow_non_contiguous=True).then_inc(mlp_in, 16)
                    sp.dma_start(w1_ids[:], w1_row_ids).then_inc(w1_ids_in, 16)
                    sp.dma_start(dense_all[:], dense_ctx.rearrange("(s p) f -> p s f", p=P)).then_inc(dense_in, 16)
                if c >= 1:
                    sp.wait_ge(wlo_done, c)
                    sp.dma_start(w_split[c - 1], w_ring[:, (c - 1) % W_SLOTS, :].bitcast(F32)).then_inc(
                        w_out[(c - 1) % W_SLOTS], 16)
            for s in range(W_SLOTS):
                sp.wait_ge(w_out[s], 16 * (CHUNKS // W_SLOTS))
            with sp.Fori(1, NB) as b:
                for c in range(CHUNKS):
                    freed = NT * b + CHUNK * (c + 1 - W_SLOTS)
                    sp.wait_ge(mains_done, freed)
                    sp.dma_start(w_ring[:, c % W_SLOTS, :].bitcast(F32), w_split[c]).then_inc(
                        w_in[c % W_SLOTS], 16)

        @block.gpsimd
        def _(pool):
            nc.gpsimd.memset(ident[:], 0.0).then_inc(ident_zero, 1)
            pool.wait_ge(ident_zero, 1)
            nc.gpsimd.affine_select(out=ident[:], in_=ident[:], compare_op=ALU.not_equal, fill=1.0,
                                    base=0, pattern=[[-1, P]], channel_multiplier=1).then_inc(ident_done, 1)

            def copy_ids(b, half):
                nc.gpsimd.tensor_copy(
                    ids_blk[half][:],
                    ids_all[:, bass.ds(b * SUB, SUB), (1 - half) * FIELDS // 2:(2 - half) * FIELDS // 2],
                ).then_inc(ids_copied, 1)
                pool.wait_ge(ids_copied, 2 * b + half + 1)

            def gather(n, par):
                m = DUOS - 1 - n
                half = n // (DUOS // 2)
                f = 2 * m + par
                at = f - (1 - half) * FIELDS // 2
                for s in range(SUB):
                    nc.gpsimd.indirect_dma_start(
                        rows[:, m, s, par * DIM:(par + 1) * DIM], None, tables[f],
                        bass.IndirectOffsetOnAxis(ap=ids_blk[half][:, s, at:at + 1], axis=0),
                    ).then_inc(rows_in[m], 16)

            def low_half(b, n):
                pool.wait_ge(hi_done, DUOS * b + n + 1)
                x = x_stack[0:DIM, 2 * (n % STACK_DUOS)]
                nc.gpsimd.tensor_tensor(x[:, 1, :], x_exact[0:DIM, n, :], x[:, 0, :].bitcast(F32),
                                        ALU.subtract).then_inc(lo_done, 1)

            def gather_next(b, n, uses):
                if n % (DUOS // 2) == 0:
                    half = n // (DUOS // 2)
                    for k in range(DUOS // 2):
                        pool.wait_ge(rows_in[DUOS - 1 - half * (DUOS // 2) - k], 2 * SUB * 16 * b)
                    copy_ids(b, half)
                pool.wait_ge(turned, turns_before(b - 1) + uses["duo", n] + 1)
                pool.sem_inc(rows_free, 1)
                gather(n, 1)
                gather(n, 0)

            pool.wait_ge(ids_in, 16)
            for k in range(DUOS + AHEAD + 1):
                if k < DUOS:
                    if k % (DUOS // 2) == 0:
                        copy_ids(0, k // (DUOS // 2))
                    gather(k, 1)
                elif k < DUOS + AHEAD:
                    gather_next(1, k - DUOS, uses_first)
                for n in LOW_AT.get(k, []):
                    low_half(0, n)
                if k < DUOS:
                    gather(k, 0)
                if k == 4:
                    pool.wait_ge(w1_ids_in, 16)
                    for kk in range(ZK):
                        nc.gpsimd.indirect_dma_start(
                            w1_sb[:, kk, :], None, W_top1,
                            bass.IndirectOffsetOnAxis(ap=w1_ids[:, kk:kk + 1], axis=0)).then_inc(w1_in, 16)

            def rest_of_block(b, n, uses_before):
                low_half(b, n)
                if 0 <= n - 6 < DUOS - AHEAD:
                    gather_next(b, n - 6 + AHEAD, uses_before)

            def next_block(b, n, uses):
                for k in range(DUOS - AHEAD + 6, n + 1)[-1:]:
                    first = 2 * (k - (DUOS - AHEAD + 6))
                    for nxt in range(first, min(first + 2, AHEAD)):
                        gather_next(b + 1, nxt, uses)

            for n in range(DUOS):
                rest_of_block(1, n, uses_first)
                next_block(1, n, uses_later)
            with pool.Fori(2, NB - 1) as b:
                for n in range(DUOS):
                    rest_of_block(b, n, uses_later)
                    next_block(b, n, uses_later)
            for n in range(DUOS):
                rest_of_block(NB - 1, n, uses_later)

        @block.tensor
        def _(pe):
            def turn_bank(b, use):
                if not (isinstance(b, int) and b == 0 and use == 0):
                    pe.wait_ge(turn_read, turns_before(b) + use)
                return turn_ps

            def duo(b, n, use):
                m = DUOS - 1 - n
                bank = turn_bank(b, use)
                pe.wait_ge(rows_in[m], 2 * SUB * 16 * (b + 1))
                for s in range(SUB):
                    op = pe.transpose(bank[:, s * P:(s + 1) * P], rows[:, m, s, :], ident[:])
                op.then_inc(turned, 1)

            def main(b, g, uses):
                first = isinstance(b, int)
                for t in range(GROUP * g, GROUP * g + GROUP):
                    i, m = TILES[t]
                    c = t // CHUNK
                    q = t // 2
                    if t % CHUNK == 0:
                        if first:
                            pe.wait_ge(whi_done, c + 1)
                            pe.wait_ge(wlo_done, c + 1)
                        else:
                            pe.wait_ge(w_in[c % W_SLOTS],
                                       b * (16 * CHUNKS // W_SLOTS) + 16 * (c // W_SLOTS + 1 - CHUNKS // W_SLOTS))
                    n = DUOS - 1 - i // 2
                    if t == duo_tiles_before(n):
                        pe.wait_ge(stack_done, DUOS * b + n + 1)
                    if t % 2 == 0 and q >= U_SLOTS:
                        pe.wait_ge(prods_done, PAIRS2 * b + q - U_SLOTS + 1)
                    elif t % 2 == 0 and not first:
                        held = max(h for h in range(PAIRS2) if h % U_SLOTS == q)
                        pe.wait_ge(prods_done, PAIRS2 * b + held - PAIRS2 + 1)
                    slot, pos = weight_place(t)
                    w = w_ring[:, slot, pos * P:(pos + 1) * P]
                    x = x_stack[:, 2 * (n % STACK_DUOS) + i % 2]
                    u = u_ps[:, 2 * (q % U_SLOTS) + t % 2, :]
                    pe.matmul(u, w, x[:, 0, :], start=True, stop=False)
                    pe.matmul(u, w, x[:, 1, :], start=False, stop=True).then_inc(mains_done, 1)

            def sums(b, g):
                first = isinstance(b, int)
                for t in range(GROUP * g, GROUP * g + GROUP):
                    i, m = TILES[t]
                    k, strip, row = z_place(t)
                    if t % 2 == 0:
                        pe.wait_ge(prods_done, PAIRS2 * b + t // 2 + 1)
                    if t == 64 * k and not (first and k == 0):
                        pe.wait_ge(z_read, ZK * b + k)
                    ones = ones_odd if i == 2 * m else ones_both
                    strips = 4 if k < ZK - 1 else 3
                    r = t - 64 * k
                    tiles = 64 if k < ZK - 1 else Z_LAST
                    op = pe.matmul(z_ps[32 * strip:32 * strip + 32, :], ones[:, 30 - row:62 - row],
                                   prod[:, t // 2 % PROD_SLOTS, t % 2, :],
                                   start=(r < strips), stop=(r >= tiles - strips))
                op.then_inc(sums_done, 1)

            def mlp(b, ev, use):
                bank = turn_bank(b, use)
                if ev[0] == "l1":
                    if ev[1] == 0:
                        pe.wait_ge(z_read, ZK * b)
                        pe.wait_ge(w1_in, 16 * ZK)
                        pe.wait_ge(mlp_in, 64)
                    cols = slice(ev[1] * P, (ev[1] + 1) * P)
                    for k in range(ZK):
                        op = pe.matmul(bank[:], w1_sb[:, k, cols], z_sb[:, k, :], start=(k == 0), stop=(k == ZK - 1))
                elif ev[0] == "l2":
                    cols = slice(ev[1] * P, (ev[1] + 1) * P)
                    for k in range(M1):
                        op = pe.matmul(bank[:], w2_sb[:, k, cols], h1_sb[:, k, :], start=(k == 0), stop=(k == M1 - 1))
                else:
                    for k in range(M2):
                        op = pe.matmul(bank[0:1, :], w3_sb[:, k:k + 1], h2_sb[:, k, :],
                                       start=(k == 0), stop=(k == M2 - 1))
                op.then_inc(turned, 1)

            def dense(b, use):
                bank = turn_bank(b, use)
                pe.wait_ge(dense_copied, b + 1)
                for s in range(SUB):
                    op = pe.transpose(bank[0:N_DENSE, s * P:(s + 1) * P], dense_blk[:, s, :], ident[:])
                op.then_inc(turned, 1)

            def run_block(b, order, uses):
                for ev in order:
                    if ev[0] == "duo":
                        duo(b, ev[1], uses[ev])
                    elif ev[0] == "main":
                        main(b, ev[1], uses)
                    elif ev[0] == "sum":
                        sums(b, ev[1])
                    elif ev[0] == "dense":
                        dense(b, uses[ev])
                    elif ev[0] != "stack":
                        mlp(b, ev, uses[ev])

            pe.wait_ge(ident_done, 1)
            pe.wait_ge(ones_done, 1)
            run_block(0, order_first, uses_first)
            with pe.Fori(1, NB) as b:
                run_block(b, order_later, uses_later)
            for ev in LAST_MLP:
                mlp(NB, ev, uses_last[ev])

        @block.vector
        def _(dve):
            nc.vector.memset(ones_both[:], 0.0)
            nc.vector.memset(z_sb[DENSE_ROW:P, ZK - 1, :], 0.0).then_inc(ones_zero, 1)
            nc.vector.memset(ones_odd[:], 0.0).then_inc(ones_zero, 1)
            dve.wait_ge(ones_zero, 2)
            nc.vector.memset(ones_both[0:DIM, 30:31], 1.0)
            nc.vector.memset(ones_both[DIM:P, 31:32], 1.0)
            nc.vector.memset(ones_odd[DIM:P, 31:32], 1.0).then_inc(ones_done, 1)

            def weight_low(c):
                dve.wait_ge(whi_done, c + 1)
                slot = w_ring[:, c % W_SLOTS, :]
                nc.vector.tensor_tensor(slot[DIM:P], raw[:, c % 2, :], slot[0:DIM].bitcast(F32),
                                        ALU.subtract).then_inc(wlo_done, 1)

            def low_half_odd(b, n):
                dve.wait_ge(hi_done, DUOS * b + n + 1)
                x = x_stack[DIM:P, 2 * (n % STACK_DUOS) + 1]
                nc.vector.tensor_tensor(x[:, 0, :], x_exact[DIM:P, n, :], x[:, 1, :].bitcast(F32),
                                        ALU.subtract).then_inc(lo_odd_done, 1)

            def products(b, q, uses):
                first = isinstance(b, int)
                t = 2 * q
                for tt in (t, t + 1):
                    n = DUOS - 1 - TILES[tt][1]
                    if TILES[tt][0] == 2 * TILES[tt][1]:
                        dve.wait_ge(turn_read, turns_before(b) + uses["duo", n] + 1)
                dve.wait_ge(mains_done, NT * b + t + 2)
                if not (first and q < PROD_SLOTS):
                    dve.wait_ge(sums_done, GROUPS * b + (t - 2 * PROD_SLOTS) // GROUP + 1)
                n0, n1 = (DUOS - 1 - TILES[tt][1] for tt in (t, t + 1))
                bank = 2 * (q % U_SLOTS)
                if n1 == n0 + 1:
                    op = nc.vector.tensor_tensor(prod[:, q % PROD_SLOTS], u_ps[:, bank:bank + 2, :],
                                                 x_exact[:, n0:n0 + 2, :], ALU.mult)
                else:
                    nc.vector.tensor_tensor(prod[:, q % PROD_SLOTS, 0], u_ps[:, bank, :], x_exact[:, n0, :], ALU.mult)
                    op = nc.vector.tensor_tensor(prod[:, q % PROD_SLOTS, 1], u_ps[:, bank + 1, :],
                                                 x_exact[:, n1, :], ALU.mult)
                op.then_inc(prods_done, 1)

            def run_block(b, uses):
                for q in range(PAIRS2):
                    if 2 * q % GROUP == 0:
                        g = 2 * q // GROUP
                        if isinstance(b, int):
                            for c in WEIGHTS_AT.get(g, []):
                                weight_low(c)
                        for n in DUO_AT.get(g, []):
                            if n >= 1:
                                low_half_odd(b, n)
                    products(b, q, uses)

            run_block(0, uses_first)
            with dve.Fori(1, NB) as b:
                run_block(b, uses_later)

        @block.scalar
        def _(act):
            def weight_high(c):
                act.wait_ge(raw_in[c % 2], 16 * RAW_DMAS[c])
                if c >= W_SLOTS:
                    act.wait_ge(mains_done, CHUNK * (c - W_SLOTS + 1))
                    act.wait_ge(w_out[c % W_SLOTS], 16 * (c // W_SLOTS))
                nc.scalar.copy(w_ring[0:DIM, c % W_SLOTS, :], raw[:, c % 2, :]).then_inc(whi_done, 1)

            def turn_bank(b, use):
                act.wait_ge(turned, turns_before(b) + use + 1)
                return turn_ps

            def duo(b, n, use):
                first = isinstance(b, int)
                bank = turn_bank(b, use)
                if not first:
                    t = FIRST_TILE[0] + n
                    act.wait_ge(prods_done, PAIRS2 * (b - 1) + t // 2 + 1)
                nc.scalar.copy(x_exact[:, n, :], bank[:]).then_inc(turn_read, 1)
                if n >= STACK_DUOS:
                    act.wait_ge(mains_done, NT * b + duo_tiles_before(n - STACK_DUOS + 1))
                elif not first:
                    held = max(h for h in range(DUOS) if h % STACK_DUOS == n)
                    act.wait_ge(mains_done, NT * (b - 1) + duo_tiles_before(held + 1))
                act.wait_ge(turn_read, turns_before(b) + use + 1)
                for f in fields_of(n):
                    at, hi = (slice(0, DIM), 0) if f % 2 == 0 else (slice(DIM, P), 1)
                    x = x_stack[:, 2 * (n % STACK_DUOS) + f % 2]
                    op = nc.scalar.copy(x[at, hi, :], x_exact[at, n, :])
                op.then_inc(hi_done, 1)
                for f in fields_of(n):
                    at, to, hi = (slice(0, DIM), slice(DIM, P), 0) if f % 2 == 0 else (slice(DIM, P), slice(0, DIM), 1)
                    x = x_stack[:, 2 * (n % STACK_DUOS) + f % 2]
                    nc.scalar.copy(x[to, 1 - hi, :], x_exact[at, n, :])

            def stack(b, n):
                act.wait_ge(lo_done, DUOS * b + n + 1)
                if n >= 1:
                    act.wait_ge(lo_odd_done, (DUOS - 1) * b + n)
                for f in fields_of(n):
                    at, to, hi = (slice(0, DIM), slice(DIM, P), 0) if f % 2 == 0 else (slice(DIM, P), slice(0, DIM), 1)
                    x = x_stack[:, 2 * (n % STACK_DUOS) + f % 2]
                    op = nc.scalar.copy(x[to, hi, :], x[at, 1 - hi, :])
                op.then_inc(stack_done, 1)

            def move_z(b, k):
                act.wait_ge(sums_done, GROUPS * b + min(K_GROUPS * (k + 1), GROUPS))
                rows_used = P if k < ZK - 1 else DENSE_ROW
                nc.scalar.copy(z_sb[0:rows_used, k, :], z_ps[0:rows_used, :]).then_inc(z_read, 1)

            def mlp(b, ev, use):
                bank = turn_bank(b, use)
                if ev[0] == "l1":
                    if ev[1] == 0:
                        act.wait_ge(wlo_done, CHUNKS)
                    nc.scalar.activation(h1_sb[:, ev[1], :], bank[:], ACT.Relu,
                                         bias=b1_sb[:, ev[1]:ev[1] + 1]).then_inc(turn_read, 1)
                elif ev[0] == "l2":
                    nc.scalar.activation(h2_sb[:, ev[1], :], bank[:], ACT.Relu,
                                         bias=b2_sb[:, ev[1]:ev[1] + 1]).then_inc(turn_read, 1)
                else:
                    nc.scalar.copy(y_row[0:1, :], bank[0:1, :]).then_inc(turn_read, 1)
                    act.wait_ge(turn_read, turns_before(b) + use + 1)
                    act.dma_start(out.rearrange("n o -> o n")[:, bass.ds((b - 1) * BLOCK, BLOCK)],
                                  y_row[0:1, :]).then_inc(y_out, 16)

            def dense(b, use):
                bank = turn_bank(b, use)
                if not isinstance(b, int):
                    act.wait_ge(y_out, 16 * b)
                nc.scalar.copy(z_sb[DENSE_ROW:DENSE_ROW + N_DENSE, ZK - 1, :], bank[0:N_DENSE]).then_inc(turn_read, 1)

            def copy_dense(b):
                if not isinstance(b, int):
                    act.wait_ge(turned, turns_before(b))
                nc.scalar.copy(dense_blk[:], dense_all[:, bass.ds(b * SUB, SUB), :]).then_inc(dense_copied, 1)

            def run_block(b, order, uses):
                for ev in order:
                    if ev[0] == "duo":
                        duo(b, ev[1], uses[ev])
                    elif ev[0] == "stack":
                        stack(b, ev[1])
                    elif ev[0] == "main":
                        if isinstance(b, int):
                            for c in WEIGHTS_AT.get(ev[1] + 1, []):
                                weight_high(c)
                        if ev[1] == 6:
                            copy_dense(b)
                    elif ev[0] == "sum":
                        g = ev[1]
                        if g % K_GROUPS == K_GROUPS - 1 or g == GROUPS - 1:
                            move_z(b, g // K_GROUPS)
                    elif ev[0] == "dense":
                        dense(b, uses[ev])
                    else:
                        mlp(b, ev, uses[ev])

            for c in WEIGHTS_AT[0]:
                weight_high(c)
            act.wait_ge(dense_in, 16)
            act.wait_ge(mlp_in, 64)
            act.wait_ge(ones_zero, 2)
            run_block(0, order_first, uses_first)
            with act.Fori(1, NB) as b:
                run_block(b, order_later, uses_later)
            for ev in LAST_MLP:
                mlp(NB, ev, uses_last[ev])
            act.wait_ge(y_out, 16 * NB)


WEIGHTS_AT = {}
for _c in range(CHUNKS):
    WEIGHTS_AT.setdefault(max(0, _c - W_SLOTS + 2), []).append(_c)
_dmas = [len(chunk_segments(c)) for c in range(CHUNKS)]
for _c in range(CHUNKS):
    for _pos, _i, _m, _n in chunk_segments(_c):
        if _i == 0 and _m == 0:
            _dmas[_c] += 1
RAW_DMAS = [sum(_dmas[c % 2:c + 1:2]) for c in range(CHUNKS)]
LAST_MLP = [("l1", 0), ("l1", 1), ("l1", 2), ("l1", 3), ("l2", 0), ("l2", 1), ("l3", 0)]


def kernel(**inputs):
    import concourse.bacc as bacc
    from concourse.bass_utils import run_bass_kernel_spmd

    nc = bacc.Bacc("TRN2", target_bir_lowering=False, num_devices=1)
    arrays = {}

    def dram(name, a):
        arrays[name] = np.ascontiguousarray(a)
        return nc.dram_tensor(name, a.shape, mybir.dt.from_np(arrays[name].dtype), kind="ExternalInput").ap()

    args = {k: dram("in_" + k, np.asarray(v)) for k, v in inputs.items()}
    tables = [args[f"tbl_{f}"] for f in range(FIELDS)]
    rows = dram("w1_row_ids", w1_rows(args["dense_ctx"].shape[1]))
    out = nc.dram_tensor("out_y", (args["dense_ctx"].shape[0], 1), F32, kind="ExternalOutput").ap()
    dlrm_tower(nc, args["dense_ctx"], args["ids"], tables, args["W_top1"], args["b_top1"], args["W_top2"],
               args["b_top2"], args["W_top3"], args["L0_rec_W"], rows, out)
    r = run_bass_kernel_spmd(nc, [arrays], core_ids=[0])
    return r.results[0]["out_y"]
```

```python
from contextlib import ExitStack

import concourse.bass as bass
import numpy as np
from concourse import mybir

ALU = mybir.AluOpType
ACT = mybir.ActivationFunctionType
F32 = mybir.dt.float32
F32R = mybir.dt.float32r
I32 = mybir.dt.int32

P = 128
FIELDS, DIM = 40, 64
DUOS = FIELDS // 2
BLOCK = 512
SUB = BLOCK // P
CHUNK = 8
W_SLOTS = 5
W_AHEAD = TAIL = 2
STACK_DUOS = 4
ROW_SLOTS = 10
U_SLOTS = 3
PROD_SLOTS = 8
LOOK = 3
LOOK_FIRST = [1] * 8 + [2] * 12
LOW_LAG = 1
VECTOR_LOWS = 6
EARLY = 3

TILES = [(i, m) for i in range(FIELDS - 2, -1, -1) for m in range(DUOS - 1, (i + 1) // 2 - 1, -1)]
NT = len(TILES)
GROUP = 8
GROUPS = NT // GROUP
PAIRS2 = NT // 2
CHUNKS = NT // CHUNK
K_GROUPS = 64 // GROUP
ZK = -(-NT // 64)
Z_LAST = NT - 64 * (ZK - 1)
DENSE_ROW = 96
FIRST_TILE = {i: min(t for t, (f, _) in enumerate(TILES) if f == i) for i in range(FIELDS - 1)}
LAST_TILE = {i: max(t for t, (f, _) in enumerate(TILES) if f == i) for i in range(FIELDS - 1)}


def pair_index(i, j):
    return i * (2 * FIELDS - i - 1) // 2 + j - i - 1


def z_place(t):
    k, r = divmod(t, 64)
    strips = 4 if k < ZK - 1 else 3
    return k, r % strips, 2 * (r // strips)


def duo_tiles_before(n):
    return n * n


def w1_rows(n_dense):
    rows = np.zeros((P, ZK), np.int32)
    for t, (i, m) in enumerate(TILES):
        k, strip, r = z_place(t)
        for par in range(2):
            j = 2 * m + par
            if j > i:
                rows[32 * strip + r + par, k] = pair_index(i, j)
    n_pairs = FIELDS * (FIELDS - 1) // 2
    rows[DENSE_ROW:DENSE_ROW + n_dense, ZK - 1] = n_pairs + np.arange(n_dense)
    return rows


def chunk_segments(c):
    out, t = [], CHUNK * c
    while t < CHUNK * (c + 1):
        i = TILES[t][0]
        n = min(LAST_TILE[i] + 1, CHUNK * (c + 1)) - t
        m_low = TILES[t + n - 1][1]
        out.append((t - CHUNK * c, i, m_low, n))
        t += n
    return out


def weight_place(t):
    c = t // CHUNK
    for pos, i, m_low, n in chunk_segments(c):
        if TILES[t][0] == i:
            return c % W_SLOTS, pos + TILES[t][1] - m_low
    raise AssertionError


def duos_at(first):
    at = {}
    for n in range(EARLY, DUOS):
        look = LOOK if not first else LOOK_FIRST[n]
        g = max(0, duo_tiles_before(n) // GROUP - look)
        if n >= STACK_DUOS:
            g = max(g, (duo_tiles_before(n - STACK_DUOS + 1) - 1) // GROUP + 1)
        assert g <= duo_tiles_before(n) // GROUP
        at.setdefault(g, []).append(n)
    return at


LOW_AT = {}
for _n in range(VECTOR_LOWS, DUOS):
    _k = min(max(_n + 1, 4 + duo_tiles_before(_n) // 12), _n + ROW_SLOTS - 1)
    LOW_AT.setdefault(_k, []).append(_n)
GATHERS_AT = {6: [10], 7: [11], 8: [12], 9: [13], 10: [14], 11: [15], 12: [16, 17], 13: [18, 19],
              14: [0, 1], 15: [2, 3], 16: [4, 5], 17: [6], 18: [7], 19: [8, 9]}


def order_of_period(first=False, last=False):
    mlp_at = {0: ("l1", 0, -1), 2: ("l1", 1, -1), 3: ("l1", 2, -1), 4: ("l1", 3, -1),
              5: ("l2", 0, -1), 6: ("l2", 1, -1), 8: ("l3", 0, -1)}
    g1, g2 = GROUPS - 2, GROUPS - 1
    if first:
        out = [("duo", 0, 0), ("duo", 1, 0), ("duo", 2, 0)]
    else:
        out = [("duo", 0, 0), ("main", g1, -1), ("duo", 1, 0), ("sum", g1 - 1, -1), ("duo", 2, 0),
               ("main", g2, -1), ("sum", g1, -1), ("sum", g2, -1)]
    if last:
        return [ev for ev in out if ev[0] != "duo"] + [mlp_at[k] for k in sorted(mlp_at)]
    for g in range(GROUPS - TAIL):
        duos = [("duo", n, 0) for n in duos_at(first).get(g, [])]
        out += duos[:1] + [("main", g, 0)] + duos[1:]
        if not first and g in mlp_at:
            out.append(mlp_at[g])
        if g:
            out.append(("sum", g - 1, 0))
        if g == GROUPS - 10:
            out.append(("dense", 0, 0))
    return out


def is_first(b):
    return isinstance(b, int) and b == 0


def fields_of(n):
    m = DUOS - 1 - n
    return [f for f in (2 * m + 1, 2 * m) if f < FIELDS - 1]


def odd_lows_at(order):
    at = {}
    for k, (what, n, _) in enumerate(order):
        if what == "duo":
            _, g, before = next(ev for ev in order[k:] if ev[0] == "main")
            pair = LOW_LAG
            if not before:
                pair = max(0, min(pair, (duo_tiles_before(n) - GROUP * g) // 2 - 1))
            at.setdefault((g, before, pair), []).append(n)
    return at


def turn_uses(order):
    events = [ev for ev in order if ev[0] in ("duo", "l1", "l2", "l3", "dense")]
    return {ev: u for u, ev in enumerate(events)}


def dlrm_tower(nc, dense_ctx, ids, tables, W_top1, b_top1, W_top2, b_top2, W_top3, W_pair,
               w1_row_ids, out):
    BATCH, N_DENSE = dense_ctx.shape
    H1, H2 = W_top2.shape
    M1, M2 = H1 // P, H2 // P
    NB = BATCH // BLOCK
    NS = BATCH // P
    assert M1 == 4 and M2 == 2 and GROUPS * GROUP == NT and CHUNKS * CHUNK == NT

    order_first, order_later, order_last = (order_of_period(first=True), order_of_period(),
                                            order_of_period(last=True))
    uses_first, uses_later, uses_last = map(turn_uses, (order_first, order_later, order_last))
    n_first, n_later = len(uses_first), len(uses_later)

    def moves(b, n):
        of_slot = [len(fields_of(k)) for k in range(n % STACK_DUOS, DUOS, STACK_DUOS)]
        return 2 * 16 * (sum(of_slot) * b + sum(of_slot[:n // STACK_DUOS + 1]))

    def turns_before(b):
        return 0 if is_first(b) else b * n_later + (n_first - n_later)

    with ExitStack() as ctx:
        def sb(name, shape, dt=F32):
            return ctx.enter_context(nc.sbuf_tensor(name, shape, dt))

        def psum(name, shape):
            return ctx.enter_context(nc.psum_tensor(name, shape, F32))

        def sem(name):
            return ctx.enter_context(nc.semaphore(name))

        u_ps = psum("u_ps", [P, 2 * U_SLOTS, BLOCK])
        z_ps = psum("z_ps", [P, BLOCK])
        turn_ps = psum("turn_ps", [P, BLOCK])

        rows = sb("rows", [P, ROW_SLOTS, SUB, P])
        x_exact = sb("x_exact", [P, DUOS, BLOCK])
        x_stack = sb("x_stack", [P, 2 * STACK_DUOS, 2, BLOCK], F32R)
        w_ring = sb("w_ring", [P, W_SLOTS, CHUNK * P], F32R)
        raw_or_h1 = sb("raw_or_h1", [P, 4, BLOCK])
        prod = sb("prod", [P, PROD_SLOTS, 2, BLOCK])
        z_sb = sb("z_sb", [P, ZK, BLOCK])
        h2_sb = sb("h2_sb", [P, M2, BLOCK])
        y_row = sb("y_row", [P, BLOCK])
        w1_sb = sb("w1_sb", [P, ZK, H1])
        w2_sb = sb("w2_sb", [P, M1, H2])
        w3_sb = sb("w3_sb", [P, M2])
        b1_sb = sb("b1_sb", [P, M1])
        b2_sb = sb("b2_sb", [P, M2])
        ident = sb("ident", [P, P])
        ones_both = sb("ones_both", [P, 62])
        ones_odd = sb("ones_odd", [P, 62])
        dense_all = sb("dense_all", [P, NS, N_DENSE])
        dense_blk = sb("dense_blk", [P, SUB, N_DENSE])
        ids_all = sb("ids_all", [P, NS, FIELDS], I32)
        ids_blk = [sb(f"ids_blk{h}", [P, SUB, FIELDS // 2], I32) for h in range(2)]
        w1_ids = sb("w1_ids", [P, ZK], I32)
        raw = raw_or_h1[0:DIM].rearrange("p a b -> p (a b)").rearrange("p (s c) -> p s c", s=2)
        h1_sb = raw_or_h1

        w_split = nc.dram_tensor("w_split", (CHUNKS, P, CHUNK * P), F32, kind="Internal").ap()

        ids_in = sem("ids_in")
        w1_ids_in = sem("w1_ids_in")
        dense_in = sem("dense_in")
        mlp_in = sem("mlp_in")
        w1_in = sem("w1_in")
        rows_in = [sem(f"rows_in{s}") for s in range(ROW_SLOTS)]
        raw_in = [sem(f"raw_in{s}") for s in range(2)]
        w_in = [sem(f"w_in{s}") for s in range(W_SLOTS)]
        w_out = [sem(f"w_out{s}") for s in range(W_SLOTS)]
        ids_copied = sem("ids_copied")
        rows_free = sem("rows_free")
        ident_zero = sem("ident_zero")
        ident_done = sem("ident_done")
        ones_zero = sem("ones_zero")
        ones_done = sem("ones_done")
        whi_done = sem("whi_done")
        wlo_done = sem("wlo_done")
        hi_done = sem("hi_done")
        lo_done = sem("lo_done")
        lo_odd_done = sem("lo_odd_done")
        dense_copied = sem("dense_copied")
        stacked = [sem(f"stacked{s}") for s in range(STACK_DUOS)]
        turned = sem("turned")
        turn_read = sem("turn_read")
        mains_done = sem("mains_done")
        prods_done = sem("prods_done")
        sums_done = sem("sums_done")
        z_read = sem("z_read")
        y_done = sem("y_done")
        y_out = sem("y_out")

        block = ctx.enter_context(nc.Block())

        @block.sync
        def _(sp):
            sp.dma_start(ids_all[:], ids.rearrange("(s p) f -> p s f", p=P)).then_inc(ids_in, 16)

            def load_raw(c):
                for pos, i, m_low, n in chunk_segments(c):
                    dst = raw[:, c % 2, pos * P:(pos + n) * P].rearrange("d (q e) -> d q e", e=DIM)
                    first, skip = 2 * m_low, 0
                    if first == i == 0:
                        sp.dma_start(dst[:, 0], W_pair[0]).then_inc(raw_in[c % 2], 16)
                        first, skip = 1, 1
                    lo = pair_index(i, first)
                    sp.dma_start(dst[:, skip:], W_pair[lo:lo + 2 * n - skip].rearrange(
                        "q d e -> d q e")).then_inc(raw_in[c % 2], 16)

            def load_small():
                sp.dma_start(w2_sb[:], W_top2.rearrange("(k p) n -> p k n", p=P)).then_inc(mlp_in, 16)
                sp.dma_start(w3_sb[:], W_top3.rearrange("(k p) o -> p (k o)", p=P),
                             allow_slow_non_contiguous=True).then_inc(mlp_in, 16)
                sp.dma_start(b1_sb[:], b_top1.rearrange("(m p) -> p m", p=P),
                             allow_slow_non_contiguous=True).then_inc(mlp_in, 16)
                sp.dma_start(b2_sb[:], b_top2.rearrange("(m p) -> p m", p=P),
                             allow_slow_non_contiguous=True).then_inc(mlp_in, 16)
                sp.dma_start(w1_ids[:], w1_row_ids).then_inc(w1_ids_in, 16)
                sp.dma_start(dense_all[:], dense_ctx.rearrange("(s p) f -> p s f", p=P)).then_inc(dense_in, 16)

            def pass_chunk(c):
                sp.wait_ge(wlo_done, c + 1)
                sp.sem_inc(w_in[c % W_SLOTS], 16)
                sp.dma_start(w_split[c], w_ring[:, c % W_SLOTS, :].bitcast(F32)).then_inc(w_out[c % W_SLOTS], 16)
                if c + 2 < CHUNKS:
                    load_raw(c + 2)

            def load_chunk(b, c):
                sp.wait_ge(mains_done, NT * b + CHUNK * (c + 1 - W_SLOTS))
                sp.dma_start(w_ring[:, c % W_SLOTS, :].bitcast(F32), w_split[c]).then_inc(w_in[c % W_SLOTS], 16)

            def move_across(b, n):
                def move(f, to_stack, from_stack):
                    own, other = (slice(0, DIM), slice(DIM, P)) if f % 2 == 0 else (slice(DIM, P), slice(0, DIM))
                    x = x_stack[:, 2 * (n % STACK_DUOS) + f % 2]
                    sp.dma_start(x[other, to_stack, :].bitcast(F32), x[own, from_stack, :].bitcast(F32)).then_inc(
                        stacked[n % STACK_DUOS], 16)

                sp.wait_ge(hi_done, DUOS * b + n + 1)
                for f in fields_of(n):
                    move(f, 1 - f % 2, f % 2)
                sp.wait_ge(lo_done, DUOS * b + n + 1)
                move(fields_of(n)[-1], 0, 1)
                if n >= 1:
                    sp.wait_ge(lo_odd_done, (DUOS - 1) * b + n)
                    move(fields_of(n)[0], 1, 0)

            def run_period(b, order):
                for what, n, before in order:
                    c = n + W_AHEAD
                    if what == "duo":
                        move_across(b, n)
                    elif what == "main" and is_first(b):
                        for split in WEIGHTS_AT.get(n + 1, []):
                            pass_chunk(split)
                    elif what == "main" and c < CHUNKS:
                        load_chunk(b + before, c)
                    elif what == "main" and order is not order_last:
                        load_chunk(b, c - CHUNKS)

            load_raw(0)
            load_raw(1)
            load_small()
            for c in WEIGHTS_AT[0]:
                pass_chunk(c)
            run_period(0, order_first)
            for s in range(W_SLOTS):
                sp.wait_ge(w_out[s], 16 * (CHUNKS // W_SLOTS))
            with sp.Fori(1, NB) as b:
                run_period(b, order_later)

        @block.gpsimd
        def _(pool):
            nc.gpsimd.memset(ident[:], 0.0).then_inc(ident_zero, 1)
            pool.wait_ge(ident_zero, 1)
            nc.gpsimd.affine_select(out=ident[:], in_=ident[:], compare_op=ALU.not_equal, fill=1.0,
                                    base=0, pattern=[[-1, P]], channel_multiplier=1).then_inc(ident_done, 1)

            def copy_ids(b, half):
                nc.gpsimd.tensor_copy(
                    ids_blk[half][:],
                    ids_all[:, bass.ds(b * SUB, SUB), (1 - half) * FIELDS // 2:(2 - half) * FIELDS // 2],
                ).then_inc(ids_copied, 1)
                pool.wait_ge(ids_copied, 2 * b + half + 1)

            def gather(n, par):
                half = n // ROW_SLOTS
                f = 2 * (DUOS - 1 - n) + par
                at = f - (1 - half) * FIELDS // 2
                for s in range(SUB):
                    nc.gpsimd.indirect_dma_start(
                        rows[:, n % ROW_SLOTS, s, par * DIM:(par + 1) * DIM], None, tables[f],
                        bass.IndirectOffsetOnAxis(ap=ids_blk[half][:, s, at:at + 1], axis=0),
                    ).then_inc(rows_in[n % ROW_SLOTS], 16)

            def low_half(b, n):
                pool.wait_ge(hi_done, DUOS * b + n + 1)
                x = x_stack[0:DIM, 2 * (n % STACK_DUOS)]
                nc.gpsimd.tensor_tensor(x[:, 1, :], x_exact[0:DIM, n, :], x[:, 0, :].bitcast(F32),
                                        ALU.subtract).then_inc(lo_done, 1)

            def gather_duo(b, n, uses_before, uses, between=()):
                half = n // ROW_SLOTS
                if n % ROW_SLOTS == 0:
                    if not is_first(b):
                        for s in range(ROW_SLOTS):
                            pool.wait_ge(rows_in[s], 2 * SUB * 16 * (2 * b + half - 1))
                    copy_ids(b, half)
                if half == 1:
                    pool.wait_ge(turned, turns_before(b) + uses["duo", n - ROW_SLOTS, 0] + 1)
                elif not is_first(b):
                    pool.wait_ge(turned, turns_before(b - 1) + uses_before["duo", n + ROW_SLOTS, 0] + 1)
                pool.sem_inc(rows_free, 1)
                gather(n, 1)
                for low in between:
                    if low == VECTOR_LOWS:
                        pool.wait_ge(lo_done, VECTOR_LOWS)
                    low_half(0, low)
                gather(n, 0)

            pool.wait_ge(ids_in, 16)
            for k in range(DUOS + ROW_SLOTS):
                if k < DUOS:
                    gather_duo(0, k, None, uses_first, LOW_AT.get(k, []))
                else:
                    gather_duo(1, k - DUOS, uses_first, None, LOW_AT.get(k, []))
                if k == DUOS + 1:
                    pool.wait_ge(w1_ids_in, 16)
                    for t in range(ZK):
                        nc.gpsimd.indirect_dma_start(
                            w1_sb[:, t, :], None, W_top1,
                            bass.IndirectOffsetOnAxis(ap=w1_ids[:, t:t + 1], axis=0)).then_inc(w1_in, 16)
            with pool.Fori(1, NB - 1) as b:
                for n in range(DUOS):
                    low_half(b, n)
                    for k in GATHERS_AT.get(n, []):
                        if k >= ROW_SLOTS:
                            gather_duo(b, k, uses_later, uses_later)
                        else:
                            gather_duo(b + 1, k, uses_later, uses_later)
            for n in range(DUOS):
                low_half(NB - 1, n)
                for k in GATHERS_AT.get(n, []):
                    if k >= ROW_SLOTS:
                        gather_duo(NB - 1, k, uses_later, uses_later)

        @block.tensor
        def _(pe):
            def turn_bank(b, use):
                if not (is_first(b) and use == 0):
                    pe.wait_ge(turn_read, turns_before(b) + use)
                return turn_ps

            def duo(b, n, use):
                bank = turn_bank(b, use)
                pe.wait_ge(rows_in[n % ROW_SLOTS], 2 * SUB * 16 * (2 * b + n // ROW_SLOTS + 1))
                for s in range(SUB):
                    op = pe.transpose(bank[:, s * P:(s + 1) * P], rows[:, n % ROW_SLOTS, s, :], ident[:])
                op.then_inc(turned, 1)

            def main(b, g):
                for t in range(GROUP * g, GROUP * g + GROUP):
                    i, m = TILES[t]
                    c = t // CHUNK
                    q = t // 2
                    if t % CHUNK == 0:
                        pe.wait_ge(w_in[c % W_SLOTS], b * (16 * CHUNKS // W_SLOTS) + 16 * (c // W_SLOTS + 1))
                    n = DUOS - 1 - i // 2
                    if t == duo_tiles_before(n):
                        pe.wait_ge(hi_done, DUOS * b + n + 1)
                        pe.wait_ge(lo_done, DUOS * b + n + 1)
                        if n >= 1:
                            pe.wait_ge(lo_odd_done, (DUOS - 1) * b + n)
                        pe.wait_ge(stacked[n % STACK_DUOS], moves(b, n))
                    if t % 2 == 0 and q >= U_SLOTS:
                        pe.wait_ge(prods_done, PAIRS2 * b + q - U_SLOTS + 1)
                    elif t % 2 == 0 and not is_first(b):
                        held = max(h for h in range(PAIRS2) if h % U_SLOTS == q)
                        pe.wait_ge(prods_done, PAIRS2 * b + held - PAIRS2 + 1)
                    slot, pos = weight_place(t)
                    w = w_ring[:, slot, pos * P:(pos + 1) * P]
                    x = x_stack[:, 2 * (n % STACK_DUOS) + i % 2]
                    u = u_ps[:, 2 * (q % U_SLOTS) + t % 2, :]
                    pe.matmul(u, w, x[:, 0, :], start=True, stop=False)
                    pe.matmul(u, w, x[:, 1, :], start=False, stop=True).then_inc(mains_done, 1)

            def sums(b, g):
                for t in range(GROUP * g, GROUP * g + GROUP):
                    i, m = TILES[t]
                    k, strip, row = z_place(t)
                    if t % 2 == 0:
                        pe.wait_ge(prods_done, PAIRS2 * b + t // 2 + 1)
                    if t == 64 * k and not (is_first(b) and k == 0):
                        pe.wait_ge(z_read, ZK * b + k)
                    ones = ones_odd if i == 2 * m else ones_both
                    strips = 4 if k < ZK - 1 else 3
                    r = t - 64 * k
                    tiles = 64 if k < ZK - 1 else Z_LAST
                    op = pe.matmul(z_ps[32 * strip:32 * strip + 32, :], ones[:, 30 - row:62 - row],
                                   prod[:, t // 2 % PROD_SLOTS, t % 2, :],
                                   start=(r < strips), stop=(r >= tiles - strips))
                op.then_inc(sums_done, 1)

            def mlp(b, ev, use):
                bank = turn_bank(b, use)
                if ev[0] == "l1":
                    if ev[1] == 0:
                        pe.wait_ge(w1_in, 16 * ZK)
                        pe.wait_ge(mlp_in, 64)
                    cols = slice(ev[1] * P, (ev[1] + 1) * P)
                    for k in range(ZK):
                        if ev[1] == 0 and k in (0, ZK - 1):
                            pe.wait_ge(z_read, ZK * (b - 1) + (ZK - 1 if k == 0 else ZK))
                        op = pe.matmul(bank[:], w1_sb[:, k, cols], z_sb[:, k, :], start=(k == 0), stop=(k == ZK - 1))
                elif ev[0] == "l2":
                    cols = slice(ev[1] * P, (ev[1] + 1) * P)
                    for k in range(M1):
                        op = pe.matmul(bank[:], w2_sb[:, k, cols], h1_sb[:, k, :], start=(k == 0), stop=(k == M1 - 1))
                else:
                    for k in range(M2):
                        op = pe.matmul(bank[0:1, :], w3_sb[:, k:k + 1], h2_sb[:, k, :],
                                       start=(k == 0), stop=(k == M2 - 1))
                op.then_inc(turned, 1)

            def dense(b, use):
                bank = turn_bank(b, use)
                pe.wait_ge(dense_copied, b + 1)
                for s in range(SUB):
                    op = pe.transpose(bank[0:N_DENSE, s * P:(s + 1) * P], dense_blk[:, s, :], ident[:])
                op.then_inc(turned, 1)

            def run_period(b, order, uses):
                for ev in order:
                    what, n, before = ev
                    if what == "duo":
                        duo(b, n, uses[ev])
                    elif what == "main":
                        main(b + before, n)
                    elif what == "sum":
                        sums(b + before, n)
                    elif what == "dense":
                        dense(b, uses[ev])
                    elif what in ("l1", "l2", "l3"):
                        mlp(b, ev, uses[ev])

            pe.wait_ge(ident_done, 1)
            pe.wait_ge(ones_done, 1)
            run_period(0, order_first, uses_first)
            with pe.Fori(1, NB) as b:
                run_period(b, order_later, uses_later)
            run_period(NB, order_last, uses_last)

        @block.vector
        def _(dve):
            nc.vector.memset(ones_both[:], 0.0)
            nc.vector.memset(z_sb[DENSE_ROW:P, ZK - 1, :], 0.0).then_inc(ones_zero, 1)
            nc.vector.memset(ones_odd[:], 0.0).then_inc(ones_zero, 1)
            dve.wait_ge(ones_zero, 2)
            nc.vector.memset(ones_both[0:DIM, 30:31], 1.0)
            nc.vector.memset(ones_both[DIM:P, 31:32], 1.0)
            nc.vector.memset(ones_odd[DIM:P, 31:32], 1.0).then_inc(ones_done, 1)

            def weight_low(c):
                dve.wait_ge(whi_done, c + 1)
                slot = w_ring[:, c % W_SLOTS, :]
                nc.vector.tensor_tensor(slot[DIM:P], raw[:, c % 2, :], slot[0:DIM].bitcast(F32),
                                        ALU.subtract).then_inc(wlo_done, 1)

            def low_half_even(n):
                dve.wait_ge(hi_done, n + 1)
                x = x_stack[0:DIM, 2 * (n % STACK_DUOS)]
                nc.vector.tensor_tensor(x[:, 1, :], x_exact[0:DIM, n, :], x[:, 0, :].bitcast(F32),
                                        ALU.subtract).then_inc(lo_done, 1)

            def low_half_odd(b, n):
                dve.wait_ge(hi_done, DUOS * b + n + 1)
                x = x_stack[DIM:P, 2 * (n % STACK_DUOS) + 1]
                nc.vector.tensor_tensor(x[:, 0, :], x_exact[DIM:P, n, :], x[:, 1, :].bitcast(F32),
                                        ALU.subtract).then_inc(lo_odd_done, 1)

            def products(b, q, x_ready):
                t = 2 * q
                for tt in (t, t + 1):
                    n = DUOS - 1 - TILES[tt][1]
                    if TILES[tt][0] == 2 * TILES[tt][1]:
                        dve.wait_ge(turn_read, x_ready(n))
                dve.wait_ge(mains_done, NT * b + t + 2)
                if not (is_first(b) and q < PROD_SLOTS):
                    dve.wait_ge(sums_done, GROUPS * b + (t - 2 * PROD_SLOTS) // GROUP + 1)
                n0, n1 = (DUOS - 1 - TILES[tt][1] for tt in (t, t + 1))
                bank = 2 * (q % U_SLOTS)
                if n1 == n0 + 1:
                    op = nc.vector.tensor_tensor(prod[:, q % PROD_SLOTS], u_ps[:, bank:bank + 2, :],
                                                 x_exact[:, n0:n0 + 2, :], ALU.mult)
                else:
                    nc.vector.tensor_tensor(prod[:, q % PROD_SLOTS, 0], u_ps[:, bank, :], x_exact[:, n0, :], ALU.mult)
                    op = nc.vector.tensor_tensor(prod[:, q % PROD_SLOTS, 1], u_ps[:, bank + 1, :],
                                                 x_exact[:, n1, :], ALU.mult)
                op.then_inc(prods_done, 1)

            def run_period(b, order, uses):
                lows = odd_lows_at(order)
                for what, n, before in order:
                    def x_ready(duo):
                        return turns_before(b) + (uses["duo", duo, 0] + 1 if not before else 0)

                    if what == "main":
                        for pair in range(GROUP // 2):
                            for duo in lows.get((n, before, pair), []):
                                if is_first(b) and duo < VECTOR_LOWS:
                                    low_half_even(duo)
                                if duo >= 1:
                                    low_half_odd(b, duo)
                            products(b + before, GROUP // 2 * n + pair, x_ready)
                        if is_first(b):
                            for c in WEIGHTS_AT.get(n + 1, []):
                                weight_low(c)

            for c in WEIGHTS_AT[0]:
                weight_low(c)
            run_period(0, order_first, uses_first)
            with dve.Fori(1, NB) as b:
                run_period(b, order_later, uses_later)
            run_period(NB, order_last, uses_last)

        @block.scalar
        def _(act):
            def weight_high(c):
                act.wait_ge(raw_in[c % 2], 16 * RAW_DMAS[c])
                if c >= W_SLOTS:
                    act.wait_ge(mains_done, CHUNK * (c - W_SLOTS + 1))
                    act.wait_ge(w_out[c % W_SLOTS], 16 * (c // W_SLOTS))
                nc.scalar.copy(w_ring[0:DIM, c % W_SLOTS, :], raw[:, c % 2, :]).then_inc(whi_done, 1)

            def turn_bank(b, use):
                act.wait_ge(turned, turns_before(b) + use + 1)
                return turn_ps

            def duo(b, n, use):
                first = is_first(b)
                bank = turn_bank(b, use)
                if not first:
                    t = FIRST_TILE[0] + n
                    act.wait_ge(prods_done, PAIRS2 * (b - 1) + t // 2 + 1)
                nc.scalar.copy(x_exact[:, n, :], bank[:]).then_inc(turn_read, 1)
                if n >= STACK_DUOS:
                    act.wait_ge(mains_done, NT * b + duo_tiles_before(n - STACK_DUOS + 1))
                elif not first:
                    held = max(h for h in range(DUOS) if h % STACK_DUOS == n)
                    act.wait_ge(mains_done, NT * (b - 1) + duo_tiles_before(held + 1))
                act.wait_ge(turn_read, turns_before(b) + use + 1)
                for f in fields_of(n):
                    at, hi = (slice(0, DIM), 0) if f % 2 == 0 else (slice(DIM, P), 1)
                    x = x_stack[:, 2 * (n % STACK_DUOS) + f % 2]
                    op = nc.scalar.copy(x[at, hi, :], x_exact[at, n, :])
                op.then_inc(hi_done, 1)

            def move_z(b, k):
                act.wait_ge(sums_done, GROUPS * b + min(K_GROUPS * (k + 1), GROUPS))
                rows_used = P if k < ZK - 1 else DENSE_ROW
                nc.scalar.copy(z_sb[0:rows_used, k, :], z_ps[0:rows_used, :]).then_inc(z_read, 1)

            def mlp(b, ev, use):
                bank = turn_bank(b, use)
                if ev[0] == "l1":
                    if ev[1] == 0:
                        act.wait_ge(wlo_done, CHUNKS)
                    nc.scalar.activation(h1_sb[:, ev[1], :], bank[:], ACT.Relu,
                                         bias=b1_sb[:, ev[1]:ev[1] + 1]).then_inc(turn_read, 1)
                elif ev[0] == "l2":
                    nc.scalar.activation(h2_sb[:, ev[1], :], bank[:], ACT.Relu,
                                         bias=b2_sb[:, ev[1]:ev[1] + 1]).then_inc(turn_read, 1)
                else:
                    nc.scalar.copy(y_row[0:1, :], bank[0:1, :]).then_inc(turn_read, 1)
                    act.wait_ge(turn_read, turns_before(b) + use + 1)
                    act.dma_start(out.rearrange("n o -> o n")[:, bass.ds((b - 1) * BLOCK, BLOCK)],
                                  y_row[0:1, :]).then_inc(y_out, 16)

            def dense(b, use):
                bank = turn_bank(b, use)
                if not is_first(b):
                    act.wait_ge(y_out, 16 * b)
                nc.scalar.copy(z_sb[DENSE_ROW:DENSE_ROW + N_DENSE, ZK - 1, :], bank[0:N_DENSE]).then_inc(turn_read, 1)

            def copy_dense(b):
                if not is_first(b):
                    act.wait_ge(turned, turns_before(b))
                nc.scalar.copy(dense_blk[:], dense_all[:, bass.ds(b * SUB, SUB), :]).then_inc(dense_copied, 1)

            def run_period(b, order, uses):
                for ev in order:
                    what, n, before = ev
                    if what == "duo":
                        duo(b, n, uses[ev])
                    elif what == "main":
                        if is_first(b):
                            for c in WEIGHTS_AT.get(n + 1, []):
                                weight_high(c)
                        if n == 6:
                            copy_dense(b)
                    elif what == "sum":
                        if n % K_GROUPS == K_GROUPS - 1 or n == GROUPS - 1:
                            move_z(b + before, n // K_GROUPS)
                    elif what == "dense":
                        dense(b, uses[ev])
                    else:
                        mlp(b, ev, uses[ev])

            for c in WEIGHTS_AT[0]:
                weight_high(c)
            act.wait_ge(dense_in, 16)
            act.wait_ge(mlp_in, 64)
            act.wait_ge(ones_zero, 2)
            run_period(0, order_first, uses_first)
            with act.Fori(1, NB) as b:
                run_period(b, order_later, uses_later)
            run_period(NB, order_last, uses_last)
            act.wait_ge(y_out, 16 * NB)


WEIGHTS_AT = {}
for _c in range(CHUNKS):
    WEIGHTS_AT.setdefault(max(0, _c - W_SLOTS + 2), []).append(_c)
_dmas = [len(chunk_segments(c)) for c in range(CHUNKS)]
for _c in range(CHUNKS):
    for _pos, _i, _m, _n in chunk_segments(_c):
        if _i == 0 and _m == 0:
            _dmas[_c] += 1
RAW_DMAS = [sum(_dmas[c % 2:c + 1:2]) for c in range(CHUNKS)]


def kernel(**inputs):
    import concourse.bacc as bacc
    from concourse.bass_utils import run_bass_kernel_spmd

    nc = bacc.Bacc("TRN2", target_bir_lowering=False, num_devices=1)
    arrays = {}

    def dram(name, a):
        arrays[name] = np.ascontiguousarray(a)
        return nc.dram_tensor(name, a.shape, mybir.dt.from_np(arrays[name].dtype), kind="ExternalInput").ap()

    args = {k: dram("in_" + k, np.asarray(v)) for k, v in inputs.items()}
    tables = [args[f"tbl_{f}"] for f in range(FIELDS)]
    rows = dram("w1_row_ids", w1_rows(args["dense_ctx"].shape[1]))
    out = nc.dram_tensor("out_y", (args["dense_ctx"].shape[0], 1), F32, kind="ExternalOutput").ap()
    dlrm_tower(nc, args["dense_ctx"], args["ids"], tables, args["W_top1"], args["b_top1"], args["W_top2"],
               args["b_top2"], args["W_top3"], args["L0_rec_W"], rows, out)
    r = run_bass_kernel_spmd(nc, [arrays], core_ids=[0])
    return r.results[0]["out_y"]
```
